# Optimizing a Trainium2 kernel written in Bass

```python
import numpy as np
import jax
import jax.numpy as jnp

def _softmax(x, axis=-1):
    return jax.nn.softmax(x, axis=axis)

def _gelu(x):
    return jax.nn.gelu(x, approximate=True)

def _silu(x):
    return jax.nn.silu(x)

def _sigmoid(x):
    return jax.nn.sigmoid(x)

def _layernorm(x, axis=-1, eps=1e-05):
    m = jnp.mean(x, axis=axis, keepdims=True)
    v = jnp.var(x, axis=axis, keepdims=True)
    return (x - m) / jnp.sqrt(v + eps)

def _scatter_add(tgt, idx, src, axis=0):
    return tgt.at[idx].add(src)

def _segment_sum(src, seg, n):
    return jax.ops.segment_sum(src, seg, n)
kernel_name = 'mk_gnn_resnorm_d2_gnn_r8_237d4e'

def setup_inputs(seed: int=0):
    np.random.seed(seed)
    _w = jnp.asarray

    def _rec_inputs():
        import jax
        import jax.numpy as jnp
        _gk = jax.random.key(seed)
        x = -0.000202 + 1 * jax.random.normal(jax.random.fold_in(_gk, 1), (6250, 128), jnp.float32)
        src = jax.random.randint(jax.random.fold_in(_gk, 2), (100000,), 0, 6250, jnp.int32)
        dst = jnp.minimum((6250 * jax.random.uniform(jax.random.fold_in(_gk, 3), (100000,)) ** 2.0).astype(jnp.int32), 49999)
        _o = jnp.argsort(dst, stable=True)
        src = src[_o]
        dst = dst[_o]
        edge_attr_3 = -0.000451519 + 1.00018 * jax.random.normal(jax.random.fold_in(_gk, 12), (100000, 3), jnp.float32)
        edge_weight = jax.random.uniform(jax.random.fold_in(_gk, 13), (100000,), jnp.float32, 0.0, 5)
        return (x, src, dst, edge_attr_3, edge_weight)
    x, src, dst, edge_attr_3, edge_weight = _rec_inputs()

    def _L0_gnn_setup():
        import jax, jax.numpy as jnp
        import numpy as np
        N_NODES = 6250
        N_EDGES = 200000
        CHANNELS = 128
        EXPANSION = 50
        CUTOFF = 5.0
        LOG2 = 0.6931471805599453

        def shifted_softplus(x):
            return jax.nn.softplus(x) - LOG2

        def gaussian_smearing(r, cutoff=CUTOFF, n=EXPANSION):
            centers = jnp.linspace(0.0, cutoff, n, dtype=r.dtype)
            delta = centers[1] - centers[0]
            coef = 1.0 / (2.0 * delta * delta)
            d = r[:, None] - centers[None, :]
            return jnp.exp(-coef * d * d)
        key = jax.random.key(seed)
        ks = jax.random.split(key, 12)
        C, F = (CHANNELS, EXPANSION)

        def lin(k, fan_in, shape):
            bound = 1.0 / np.sqrt(fan_in)
            return jax.random.uniform(k, shape, jnp.float32, -bound, bound)
        return {'features': jax.random.normal(ks[0], (N_NODES, C), jnp.float32), 'edge_distances': jax.random.uniform(ks[1], (N_EDGES,), jnp.float32) * CUTOFF, 'W_lin': lin(ks[2], C, (C, C)), 'Wf1': lin(ks[3], F, (F, C)), 'bf1': lin(ks[4], F, (C,)), 'Wf2': lin(ks[5], C, (C, C)), 'bf2': lin(ks[6], C, (C,)), 'Wm1': lin(ks[7], C, (C, C)), 'bm1': lin(ks[8], C, (C,)), 'Wm2': lin(ks[9], C, (C, C)), 'bm2': lin(ks[10], C, (C,)), 'senders': jax.random.randint(ks[11], (N_EDGES,), 0, N_NODES, jnp.int32), 'receivers': jax.random.randint(jax.random.fold_in(key, 99), (N_EDGES,), 0, N_NODES, jnp.int32)}
    _L0_gnn_all = _L0_gnn_setup()
    _L0_gnn_in = {k: v for k, v in _L0_gnn_all.items() if k in ('W_lin', 'Wf1', 'bf1', 'Wf2', 'bf2', 'Wm1', 'bm1', 'Wm2', 'bm2')}
    del _L0_gnn_all

    def _L1_gnn_setup():
        import jax, jax.numpy as jnp
        import numpy as np
        N = 6250
        E = 100000
        MUL = 32
        NB = 8
        R_MAX = 1.0
        AVG = 16.0
        SQ3 = 3.0 ** 0.5

        def _radial_embedding(r):
            x = jnp.clip(r / R_MAX, 0.0, 1.0)
            centers = jnp.arange(NB, dtype=jnp.float32) / (NB - 1)
            sigma = 1.0 / (NB - 1)
            emb = jnp.exp(-0.5 * ((x[:, None] - centers[None, :]) / sigma) ** 2)
            emb = emb * NB ** 0.5 * (r <= R_MAX).astype(jnp.float32)[:, None]
            return emb
        key = jax.random.key(seed)
        k = jax.random.split(key, 12)
        inp = {'node_feats': jax.random.normal(k[0], (N, 4 * MUL), dtype=jnp.float32), 'edge_vec': jax.random.normal(k[1], (E, 3), dtype=jnp.float32), 'edge_length': jax.random.uniform(k[2], (E,), dtype=jnp.float32), 'senders': jax.random.randint(k[3], (E,), 0, N, dtype=jnp.int32), 'receivers': jax.random.randint(k[4], (E,), 0, N, dtype=jnp.int32), 'num_nodes': N, 'W_up0': jax.random.normal(k[5], (MUL, MUL), dtype=jnp.float32), 'W_up1': jax.random.normal(k[6], (MUL, MUL), dtype=jnp.float32), 'mlp_w0': jax.random.normal(k[7], (NB, 64), dtype=jnp.float32) / NB ** 0.5, 'mlp_b0': jnp.zeros((64,), dtype=jnp.float32), 'mlp_w1': jax.random.normal(k[8], (64, 64), dtype=jnp.float32) / 8.0, 'mlp_b1': jnp.zeros((64,), dtype=jnp.float32), 'mlp_w2': jax.random.normal(k[9], (64, 4 * MUL), dtype=jnp.float32) / 8.0, 'mlp_b2': jnp.zeros((4 * MUL,), dtype=jnp.float32), 'W_out0': jax.random.normal(k[10], (2 * MUL, MUL), dtype=jnp.float32), 'W_out1': jax.random.normal(k[11], (2 * MUL, MUL), dtype=jnp.float32)}
        return inp
    _L1_gnn_all = _L1_gnn_setup()
    _L1_gnn_in = {k: v for k, v in _L1_gnn_all.items() if k in ('W_up0', 'W_up1', 'mlp_w0', 'mlp_b0', 'mlp_w1', 'mlp_b1', 'mlp_w2', 'mlp_b2', 'W_out0', 'W_out1')}
    del _L1_gnn_all
    return {'x': x, 'src': src, 'dst': dst, 'edge_attr_3': edge_attr_3, 'edge_weight': edge_weight, 'L0_gnn_W_lin': _L0_gnn_in['W_lin'], 'L0_gnn_Wf1': _L0_gnn_in['Wf1'], 'L0_gnn_bf1': _L0_gnn_in['bf1'], 'L0_gnn_Wf2': _L0_gnn_in['Wf2'], 'L0_gnn_bf2': _L0_gnn_in['bf2'], 'L0_gnn_Wm1': _L0_gnn_in['Wm1'], 'L0_gnn_bm1': _L0_gnn_in['bm1'], 'L0_gnn_Wm2': _L0_gnn_in['Wm2'], 'L0_gnn_bm2': _L0_gnn_in['bm2'], 'L1_gnn_W_up0': _L1_gnn_in['W_up0'], 'L1_gnn_W_up1': _L1_gnn_in['W_up1'], 'L1_gnn_mlp_w0': _L1_gnn_in['mlp_w0'], 'L1_gnn_mlp_b0': _L1_gnn_in['mlp_b0'], 'L1_gnn_mlp_w1': _L1_gnn_in['mlp_w1'], 'L1_gnn_mlp_b1': _L1_gnn_in['mlp_b1'], 'L1_gnn_mlp_w2': _L1_gnn_in['mlp_w2'], 'L1_gnn_mlp_b2': _L1_gnn_in['mlp_b2'], 'L1_gnn_W_out0': _L1_gnn_in['W_out0'], 'L1_gnn_W_out1': _L1_gnn_in['W_out1']}

def reference(x, src, dst, edge_attr_3, edge_weight, L0_gnn_W_lin, L0_gnn_Wf1, L0_gnn_bf1, L0_gnn_Wf2, L0_gnn_bf2, L0_gnn_Wm1, L0_gnn_bm1, L0_gnn_Wm2, L0_gnn_bm2, L1_gnn_W_up0, L1_gnn_W_up1, L1_gnn_mlp_w0, L1_gnn_mlp_b0, L1_gnn_mlp_w1, L1_gnn_mlp_b1, L1_gnn_mlp_w2, L1_gnn_mlp_b2, L1_gnn_W_out0, L1_gnn_W_out1):
    import jax
    import jax.numpy as jnp

    def _L0_gnn_ref(features, edge_distances, W_lin, Wf1, bf1, Wf2, bf2, Wm1, bm1, Wm2, bm2, senders, receivers):
        import jax, jax.numpy as jnp
        import numpy as np
        N_NODES = 6250
        N_EDGES = 200000
        CHANNELS = 128
        EXPANSION = 50
        CUTOFF = 5.0
        LOG2 = 0.6931471805599453

        def shifted_softplus(x):
            return jax.nn.softplus(x) - LOG2

        def gaussian_smearing(r, cutoff=CUTOFF, n=EXPANSION):
            centers = jnp.linspace(0.0, cutoff, n, dtype=r.dtype)
            delta = centers[1] - centers[0]
            coef = 1.0 / (2.0 * delta * delta)
            d = r[:, None] - centers[None, :]
            return jnp.exp(-coef * d * d)
        h = features @ W_lin.T
        basis = gaussian_smearing(edge_distances)
        ef = shifted_softplus(basis @ Wf1 + bf1) @ Wf2 + bf2
        messages = h[senders] * ef
        agg = jax.ops.segment_sum(messages, receivers, num_segments=N_NODES)
        return shifted_softplus(agg @ Wm1 + bm1) @ Wm2 + bm2

    def _L1_gnn_ref(node_feats, edge_vec, edge_length, senders, receivers, num_nodes, W_up0, W_up1, mlp_w0, mlp_b0, mlp_w1, mlp_b1, mlp_w2, mlp_b2, W_out0, W_out1):
        import jax, jax.numpy as jnp
        import numpy as np
        N = 6250
        E = 100000
        MUL = 32
        NB = 8
        R_MAX = 1.0
        AVG = 16.0
        SQ3 = 3.0 ** 0.5

        def _radial_embedding(r):
            x = jnp.clip(r / R_MAX, 0.0, 1.0)
            centers = jnp.arange(NB, dtype=jnp.float32) / (NB - 1)
            sigma = 1.0 / (NB - 1)
            emb = jnp.exp(-0.5 * ((x[:, None] - centers[None, :]) / sigma) ** 2)
            emb = emb * NB ** 0.5 * (r <= R_MAX).astype(jnp.float32)[:, None]
            return emb
        f32 = jnp.float32
        rhat = edge_vec / (jnp.linalg.norm(edge_vec, axis=-1, keepdims=True) + 1e-12)
        Y1 = SQ3 * rhat
        emb = _radial_embedding(edge_length)
        h = jax.nn.silu(emb @ mlp_w0 + mlp_b0)
        h = jax.nn.silu(h @ mlp_w1 + mlp_b1)
        w = (h @ mlp_w2 + mlp_b2).reshape(-1, 4, MUL)
        s = node_feats[:, :MUL]
        v = node_feats[:, MUL:].reshape(-1, MUL, 3)
        xs = s @ W_up0 / f32(MUL) ** 0.5
        xv = jnp.einsum('nmc,mk->nkc', v, W_up1) / f32(MUL) ** 0.5
        ss = xs[senders]
        vv = xv[senders]
        m0 = w[:, 0] * ss
        m1 = w[:, 1][:, :, None] * ss[:, :, None] * Y1[:, None, :]
        m2 = w[:, 2][:, :, None] * vv
        m3 = w[:, 3] * (jnp.einsum('emc,ec->em', vv, Y1) / SQ3)
        mid_s = jnp.concatenate([m0, m3], axis=1)
        mid_v = jnp.concatenate([m1, m2], axis=1)
        msg_s = jax.ops.segment_sum(mid_s, receivers, num_segments=num_nodes)
        msg_v = jax.ops.segment_sum(mid_v, receivers, num_segments=num_nodes)
        out_s = msg_s @ W_out0 / f32(2 * MUL) ** 0.5
        out_v = jnp.einsum('nmc,mk->nkc', msg_v, W_out1) / f32(2 * MUL) ** 0.5
        out = jnp.concatenate([out_s, out_v.reshape(-1, 3 * MUL)], axis=1)
        return out / max(AVG, 1e-08)
    x = _layernorm(x + _L0_gnn_ref(x, edge_weight, L0_gnn_W_lin, L0_gnn_Wf1, L0_gnn_bf1, L0_gnn_Wf2, L0_gnn_bf2, L0_gnn_Wm1, L0_gnn_bm1, L0_gnn_Wm2, L0_gnn_bm2, src, dst), axis=-1)
    x = _layernorm(x + _L1_gnn_ref(x, edge_attr_3, edge_weight, src, dst, 6250, L1_gnn_W_up0, L1_gnn_W_up1, L1_gnn_mlp_w0, L1_gnn_mlp_b0, L1_gnn_mlp_w1, L1_gnn_mlp_b1, L1_gnn_mlp_w2, L1_gnn_mlp_b2, L1_gnn_W_out0, L1_gnn_W_out1), axis=-1)
    return x

_drawn_inputs = setup_inputs


def setup_inputs(seed=0):
    import zlib

    import numpy as np

    out = dict(_drawn_inputs(seed))
    spreads = {'L1_gnn_mlp_b0': (0.0, 0.8), 'L1_gnn_mlp_b1': (0.0, 0.645), 'L1_gnn_mlp_b2': (0.0, 0.331)}
    factors = {'L0_gnn_Wf1': 4.781,
     'L0_gnn_bf1': 5.941,
     'L0_gnn_Wf2': 3.679,
     'L0_gnn_bf2': 2.755,
     'L0_gnn_bm1': 3.297}
    for name, (base, spread) in spreads.items():
        noise = np.random.default_rng([zlib.crc32(name.encode()), seed]).standard_normal(out[name].shape)
        drawn = base * np.exp(spread * noise) if base else spread * noise
        out[name] = jnp.asarray(drawn.astype(out[name].dtype))
    for name, factor in factors.items():
        out[name] = (out[name] * factor).astype(out[name].dtype)
    return out
```

```python
from contextlib import ExitStack
import math

import numpy as np
import concourse.bass as bass
from concourse import mybir

F32 = mybir.dt.float32
BF16 = mybir.dt.bfloat16
I32 = mybir.dt.int32
I16 = mybir.dt.int16
ALU = mybir.AluOpType
ACT = mybir.ActivationFunctionType
AXES = mybir.AxisListType

P = 128
HALF_CHUNKS = 4
HALF = HALF_CHUNKS * P
SLOTS = 4
PAIR = 2 * HALF
WINDOW = 128
UNIT_TILES = 4
LN_EPS = 1e-5
EXP_CAP = 40.0

RADIAL, CUTOFF = 50, 5.0
BESSEL = 8
MUL = 32
HIDDEN = 64
AVG_DEGREE = 16.0
SPREAD = 64


def padded_edges(edges):
    return -(-edges // (SLOTS * HALF)) * SLOTS * HALF


def pad_receiver(nodes):
    return -(-nodes // P) * P


class Counter:

    def __init__(self, eng=None, it=0):
        self.eng, self.it, self.known = eng, it, {}

    def value(self, scale, offset):
        if self.eng is None:
            return offset
        if (scale, offset) not in self.known:
            self.known[scale, offset] = self.eng.snap(self.it * scale + offset)
        return self.known[scale, offset]


class Half:

    def __init__(self, rel, count, counter=None):
        self.rel, self.count, self.counter = rel, count, counter or Counter()
        self.slot, self.pair_slot, self.parity = rel % SLOTS, rel // 2 % 2, rel % 2

    def real(self):
        return self.counter.eng is not None or 0 <= self.rel < self.count

    def before(self, k):
        return Half(self.rel - k, self.count, self.counter)

    def number(self, scale=1, plus=0):
        return self.counter.value(SLOTS * scale, self.rel * scale + plus)

    def upto(self, back=0):
        return self.counter.value(SLOTS, self.rel + 1 - back)

    def pair_upto(self, back=0):
        return self.counter.value(SLOTS // 2, self.rel // 2 + 1 - back)

    def pair(self):
        return self.counter.value(SLOTS // 2, self.rel // 2)

    def uses(self, scale, back=0):
        return self.counter.value(scale, (self.rel // SLOTS + 1 - back) * scale)


def wait(eng, sem, value):
    if not isinstance(value, int) or value > 0:
        eng.wait_ge(sem, value)


def for_halves(eng, iterations, step, behind):
    count = iterations * SLOTS
    peeled = min(2, iterations)
    for n in range(peeled * SLOTS):
        step(Half(n, count))
    if iterations > peeled:
        with eng.Fori(peeled, iterations) as it:
            counter = Counter(eng, it)
            for s in range(SLOTS):
                step(Half(s, count, counter))
    for n in range(count, count + behind):
        step(Half(n, count))


class Unit:

    def __init__(self, rel, tiles, rows, counter=None):
        self.rel, self.tiles, self.rows, self.counter = rel, tiles, rows, counter or Counter()
        self.slot = rel % 2
        self.cols = tiles * P if rows == P else rows

    def upto(self, back=0):
        return self.counter.value(2, self.rel + 1 - back)

    def uses(self, scale, back=0):
        return self.counter.value(scale, (self.rel // 2 + 1 - back) * scale)

    def tile(self, scale=1, plus=0):
        return self.counter.value(2 * UNIT_TILES * scale, self.rel * UNIT_TILES * scale + plus)


def fixed_unit(number, nodes):
    if number < 0 or number * UNIT_TILES * P >= nodes:
        return None
    left = nodes - number * UNIT_TILES * P
    tiles = min(UNIT_TILES, -(-left // P))
    assert tiles == 1 or left >= tiles * P
    return Unit(number, tiles, min(P, left))


def for_units(eng, nodes, step, behind):
    whole = nodes // (UNIT_TILES * P) // 2
    units = -(-nodes // (UNIT_TILES * P))
    peeled = min(2, whole)
    for n in range(2 * peeled):
        step(fixed_unit(n, nodes), fixed_unit(n - 1, nodes))
    if whole > peeled:
        with eng.Fori(peeled, whole) as it:
            counter = Counter(eng, it)
            for s in range(2):
                step(Unit(s, UNIT_TILES, P, counter), Unit(s - 1, UNIT_TILES, P, counter))
    for n in range(2 * whole, units + behind):
        step(fixed_unit(n, nodes), fixed_unit(n - 1, nodes))


def build(nc, x, src, dst, edge_attr, edge_weight, W_lin, Wf1, bf1, Wf2, bf2, Wm1, bm1, Wm2, bm2,
          W_up0, W_up1, mlp_w0, mlp_b0, mlp_w1, mlp_b1, mlp_w2, mlp_b2, W_out0, W_out1, out, ctx):
    nodes, chans = x.shape
    edges = src.shape[0]
    iterations = edges // (SLOTS * HALF)
    halves = iterations * SLOTS
    chunks = halves * HALF_CHUNKS
    pairs = halves // 2
    pair_chunks = PAIR // P
    tiles = -(-nodes // P)
    last_unit = -(-nodes // (UNIT_TILES * P)) - 1
    width = tiles * P + P
    all_windows = width // WINDOW
    assert chans == P and pairs <= P and all_windows % 2 == 0

    def sb(name, shape, dt=F32):
        return ctx.enter_context(nc.sbuf_tensor(name, shape, dt))

    def sem(name):
        return ctx.enter_context(nc.semaphore(name))

    def sems(name, n):
        return [sem(f"{name}{i}") for i in range(n)]

    h_dram = nc.dram_tensor("h_table", (nodes, P), F32).ap()
    v_dram = nc.dram_tensor("up_table", (nodes, P), F32).ap()
    emb_dram = nc.dram_tensor("radial_embedding", (pairs, 2 * BESSEL, HALF), F32).ap()

    x_sb = sb("x_sb", [P, tiles, P])
    sums = sb("sums", [P, 2, width])
    scratch = sums[:, 1, :]
    windows_iota = sb("windows_iota", [P, all_windows * WINDOW], I16)
    iota = sb("iota", [P, WINDOW])
    ident = sb("ident", [P, P])
    ones = sb("ones", [P, 1])
    ones_bf = sb("ones_bf", [3, P], BF16)
    eps = sb("eps", [P, 1])
    log_scale = sb("log_scale", [P, 1])
    half_const = sb("half_const", [P, 1])
    steps8 = sb("steps8", [P, BESSEL])

    W_lin_sb, W_linT = sb("W_lin_sb", [P, P]), sb("W_linT", [P, P])
    Wf1_sb = sb("Wf1_sb", [SPREAD + RADIAL, P])
    Wf2_sb, Wm1_sb, Wm2_sb = (sb(n, [P, P]) for n in ("Wf2_sb", "Wm1_sb", "Wm2_sb"))
    W_up_sb, W_outA, W_outB = (sb(n, [P, P]) for n in ("W_up_sb", "W_outA", "W_outB"))
    W_out_in = sb("W_out_in", [P, 2, MUL])
    w0_sb = sb("w0_sb", [2 * BESSEL, P])
    w1_sb = sb("w1_sb", [P, P])
    w2_sb = sb("w2_sb", [P, P])
    cols = sb("cols", [P, 6])
    bf1_c, bf1_s, bm1_c, bm1_s, b0_c, b1_c = (cols[:, i:i + 1] for i in range(6))
    brow = sb("brow", [1, 3, P])
    brest = sb("brest", [1, 3, P])
    bparts = sb("bparts", [1, 3, 3 * P], BF16)
    bias3 = sb("bias3", [3, 3, P], BF16)
    neg_centers = sb("neg_centers", [P, 1])

    src_i = sb("src_i", [pairs, PAIR], I32)
    dst_i = sb("dst_i", [pairs, PAIR], I32)
    dst_f = sb("dst_f", [pairs, PAIR])
    fits_row = sb("fits_row", [pairs, 1])
    sorted_flag = sb("sorted_flag", [1, 1], I32)
    srcT = sb("srcT", [P, pairs, pair_chunks])
    dstT = sb("dstT", [P, pairs, pair_chunks])
    relT = sb("relT", [P, pairs, pair_chunks])
    dirT = sb("dirT", [P, pairs, pair_chunks, 3])
    bases = sb("bases", [1, halves], I32)
    wt_rows = sb("wt_rows", [pairs, PAIR])
    emb_k = sb("emb_k", [pairs, 2, PAIR])
    attr = scratch[0:pairs, 0:3 * PAIR]
    attr_sq = scratch[0:pairs, 3 * PAIR:6 * PAIR]

    sent = sb("sent", [P, SLOTS, HALF_CHUNKS, P])
    picks = sb("picks", [P, 2, 2 * HALF_CHUNKS], I32)
    basis = sb("basis", [P, 2, HALF])
    soft = sb("soft", [P, 2, HALF])
    hid = sb("hid", [P, 2, HALF])
    msg = sb("msg", [P, 2, HALF_CHUNKS, 2 * P + MUL])
    dots = sb("dots", [P, 2, HALF_CHUNKS, 3, MUL])
    dot = sb("dot", [P, 2, HALF_CHUNKS, MUL])
    onehot = sb("onehot", [P, 2, HALF_CHUNKS, WINDOW])
    emb_in = sb("emb_in", [2 * BESSEL, 2, HALF])
    h1 = sb("h1", [P, 2, HALF])
    h2 = sb("h2", [P, 2, HALF])
    msg_flat = msg[:, :, :, :].rearrange("p a b c -> p (a b c)")
    fits, r_clip = msg_flat[0:pairs, 0:PAIR], msg_flat[0:pairs, PAIR:2 * PAIR]
    src_f, rel2 = emb_k[:, 0, :], emb_k[:, 1, :]
    rel_f = rel2.rearrange("g (a b) -> g a b", b=HALF)
    r_mask, norm = (h[0:pairs, :, :].rearrange("p a b -> p (a b)") for h in (h1, h2))

    unit_in = sb("unit_in", [P, 2, UNIT_TILES, P])
    unit_T = sb("unit_T", [P, 2, UNIT_TILES * P])
    unit_out = sb("unit_out", [P, 2, UNIT_TILES, P])
    stage = sent[:, :, :, :].rearrange("p (s k) j c -> p s k (j c)", k=2)
    stats = sb("stats", [P, 2, UNIT_TILES, 6])
    all_stats = sb("all_stats", [P, tiles, 6])
    moments = sb("moments", [P, 3, tiles])
    rstd = sb("rstd", [P, tiles])

    bank = [ctx.enter_context(nc.psum_tensor(f"bank{i}", [P, HALF], F32)) for i in range(8)]
    quads = [b[:, :].rearrange("p (j c) -> p j c", j=4) for b in bank]
    filtA = [bank[i] for i in (0, 1, 6, 7)]
    filtB = quads[2:4]
    winps = bank[4:6]

    s_const = sem("s_const")
    s_ident = sem("s_ident")
    s_measuring = sem("s_measuring")
    s_gathering = sem("s_gathering")
    s_pool = sem("s_pool")
    d_rows = sems("d_rows", 4)
    d_wlin, d_weights, d_bias = sem("d_wlin"), sem("d_weights"), sem("d_bias")
    d_x, d_bases, d_up = sem("d_x"), sem("d_bases"), sem("d_up")
    d_bparts = sem("d_bparts")
    s_blocks = sem("s_blocks")
    s_dve = sem("s_dve")
    s_own = sem("s_own")
    s_wT, s_wTc = sem("s_wT"), sem("s_wTc")
    s_turn, s_turned = sem("s_turn"), sem("s_turned")
    s_act = sem("s_act")
    s_weights = sem("s_weights")
    s_flag, s_fits = sem("s_flag"), sem("s_fits")
    s_emb, d_emb = sems("s_emb", 2), sems("d_emb", 2)
    s_embsq = sem("s_embsq")
    s_norm = sem("s_norm")
    s_rclip = sem("s_rclip")

    def unit_sems(phase):
        by_dma = {k: sems(f"{phase}_{k}", 2) for k in ("loaded", "stored")}
        return by_dma | {k: sem(f"{phase}_{k}") for k in
                         ("normed", "turned", "copied", "product", "ready")}

    def dense_sems(phase):
        return {k: sem(f"{phase}_{k}") for k in
                ("staged", "first", "capped", "soft_e", "soft_l", "hidden", "second", "added", "stats")}

    table0, table1 = unit_sems("tab0"), unit_sems("tab1")
    dense0, dense1 = dense_sems("den0"), dense_sems("den1")
    s_var, s_rstd = sems("s_var", 2), sems("s_rstd", 2)
    s_out = sems("s_out", 2)
    s_ynorm = sem("s_ynorm")
    s_zeroed = sem("s_zeroed")

    def edge_sems(layer):
        by_dma = {"r_in": sems(f"L{layer}_r_in", 2), "landed": sems(f"L{layer}_landed", SLOTS)}
        own = (("squared", "basis", "capped", "exped", "logged", "soft"),
               ("act1", "filt2", "act2", "dots", "scaled", "dot"))[layer]
        return by_dma | {k: sem(f"L{layer}_{k}") for k in
                         ("picked", "filt1", "filt", "msg", "window", "added") + own}

    L0, L1 = edge_sems(0), edge_sems(1)
    every = [{k: sems(f"every{n}_{k}", 2) for k in ("onehot", "window", "added")} for n in range(2)]

    block = ctx.enter_context(nc.Block())

    def at(start, size):
        return slice(start, start + size) if isinstance(start, int) else bass.ds(start, size)

    def by_chunk(tile_T, h):
        return tile_T[:, :, :].rearrange("p a b -> p (a b)")[:, at(h.number(HALF_CHUNKS), HALF_CHUNKS)]

    @block.gpsimd
    def _(pool):
        g = nc.gpsimd
        g.memset(ident[:], 0.0).then_inc(s_pool, 1)
        pool.wait_ge(s_pool, 1)
        g.affine_select(out=ident[:], in_=ident[:], compare_op=ALU.not_equal, fill=1.0, base=0,
                        pattern=[[-1, P]], channel_multiplier=1).then_inc(s_ident, 1)
        made = [0]

        def constant(ins):
            made[0] += 1
            ins.then_inc(s_const, 1)
            pool.wait_ge(s_const, made[0])

        pool.wait_ge(s_ident, 1)
        constant(g.memset(ones[:], 1.0))
        constant(g.memset(ones_bf[:], 1.0))
        constant(g.memset(eps[:], LN_EPS))
        constant(g.memset(log_scale[:], 0.5 * math.log(BESSEL)))
        constant(g.memset(half_const[:], 0.5))
        constant(g.memset(basis[:], 0.0))
        for part in (neg_centers[0:SPREAD, :], neg_centers[SPREAD:P, :]):
            constant(g.iota(part, [[0, 1]], base=0, channel_multiplier=1,
                            allow_small_or_imprecise_dtypes=True))
        for row, n in ((steps8, BESSEL), (iota, WINDOW), (windows_iota, all_windows * WINDOW)):
            constant(g.iota(row[:], [[1, n]], base=0, channel_multiplier=0,
                            allow_small_or_imprecise_dtypes=True))
        constant(g.memset(sums[:, 0, :], 0.0))

        def store_tables(sm, table):
            def step(u, _):
                if u is None:
                    return
                wait(pool, sm["ready"], u.upto())
                rows = table[at(u.tile(P), u.cols), :]
                rows = rows.rearrange("(t p) c -> p t c", p=u.rows)
                pool.dma_start(rows, unit_out[0:u.rows, u.slot, 0:u.tiles, :])\
                    .then_inc(sm["stored"][u.slot], 16)
            for_units(pool, nodes, step, 0)
            for s in range(2):
                pool.wait_ge(sm["stored"][s], 16 * (last_unit // 2 + (s <= last_unit % 2)))

        def gather(sm, table):
            def step(h):
                if h.parity == 0:
                    wait(pool, sm["picked"], h.pair_upto())
                wait(pool, sm["msg"], h.upto(SLOTS))
                pool.sem_inc(s_gathering, 1)
                for j in range(HALF_CHUNKS):
                    pick = picks[:, h.pair_slot, (h.parity) * HALF_CHUNKS + j:
                                 (h.parity) * HALF_CHUNKS + j + 1]
                    pool.indirect_dma_start(sent[:, h.slot, j, :], None, table,
                                            bass.IndirectOffsetOnAxis(pick, 0))\
                        .then_inc(sm["landed"][h.slot], 16)
            for_halves(pool, iterations, step, 0)

        store_tables(table0, h_dram)
        gather(L0, h_dram)
        pool.wait_ge(dense0["first"], last_unit + 1)
        pool.wait_ge(s_turned, 12)
        g.memset(sums[:, :, :], 0.0).then_inc(s_zeroed, 1)
        store_tables(table1, v_dram)
        gather(L1, v_dram)

    @block.sync
    def _(sp):
        sp.dma_start(src_i[:], src.rearrange("(g e) -> g e", e=PAIR)).then_inc(d_rows[0], 16)
        sp.dma_start(W_lin_sb[:], W_lin).then_inc(d_wlin, 16)

        def load_x(u, _):
            if u is None:
                return
            wait(sp, table0["turned"], u.upto(2))
            rows = x[at(u.tile(P), u.cols), :]
            sp.dma_start(unit_in[0:u.rows, u.slot, 0:u.tiles, :],
                         rows.rearrange("(t p) c -> p t c", p=u.rows))\
                .then_inc(table0["loaded"][u.slot], 16)
        for_units(sp, nodes, load_x, 0)

        sp.dma_start(dst_i[:], dst.rearrange("(g e) -> g e", e=PAIR)).then_inc(d_rows[1], 16)
        sp.dma_start(bases[:], dst.rearrange("(a n e) -> a n e", a=1, e=HALF)[:, :, 0],
                     allow_slow_non_contiguous=True)\
            .then_inc(d_bases, 16)
        for s in range(2):
            sp.dma_start(Wf1_sb[s * SPREAD:s * SPREAD + RADIAL, :], Wf1).then_inc(d_weights, 16)
        for w_sb, w in ((Wf2_sb, Wf2), (Wm1_sb, Wm1), (Wm2_sb, Wm2)):
            sp.dma_start(w_sb[:], w).then_inc(d_weights, 16)
        sp.dma_start(bf1_c, bf1.rearrange("(p a) -> p a", a=1)).then_inc(d_bias, 16)
        sp.dma_start(bm1_c, bm1.rearrange("(p a) -> p a", a=1)).then_inc(d_bias, 16)
        for s in range(2):
            sp.dma_start(b0_c[s * HIDDEN:(s + 1) * HIDDEN, :],
                         mlp_b0.rearrange("(p a) -> p a", a=1)).then_inc(d_bias, 16)
            sp.dma_start(b1_c[s * HIDDEN:(s + 1) * HIDDEN, :],
                         mlp_b1.rearrange("(p a) -> p a", a=1)).then_inc(d_bias, 16)
        for i, b in enumerate((bf2, bm2, mlp_b2)):
            sp.dma_start(brow[:, i, :], b.rearrange("(a c) -> a c", a=1)).then_inc(d_bias, 16)
        sp.dma_start(wt_rows[:], edge_weight.rearrange("(g e) -> g e", e=PAIR))\
            .then_inc(d_rows[2], 16)
        sp.dma_start(attr, edge_attr.rearrange("(g e) c -> g (e c)", e=PAIR)).then_inc(d_rows[3], 16)
        sp.wait_ge(s_blocks, 1)
        for s in range(2):
            sp.dma_start(w0_sb[s * BESSEL:(s + 1) * BESSEL, s * HIDDEN:(s + 1) * HIDDEN], mlp_w0)\
                .then_inc(d_up, 16)
            sp.dma_start(w1_sb[s * HIDDEN:(s + 1) * HIDDEN, s * HIDDEN:(s + 1) * HIDDEN], mlp_w1)\
                .then_inc(d_up, 16)
            sp.dma_start(w2_sb[s * HIDDEN:(s + 1) * HIDDEN, :], mlp_w2).then_inc(d_up, 16)
        sp.dma_start(W_up_sb[0:MUL, 0:MUL], W_up0).then_inc(d_up, 16)
        for c in range(3):
            cs = slice(MUL * (c + 1), MUL * (c + 2))
            sp.dma_start(W_up_sb[MUL + c:P:3, cs], W_up1).then_inc(d_up, 16)
            sp.dma_start(W_out_in[cs, 0, :], W_out1[MUL:2 * MUL, :]).then_inc(d_up, 16)
            sp.dma_start(W_out_in[cs, 1, :], W_out1[0:MUL, :]).then_inc(d_up, 16)
        sp.dma_start(W_out_in[0:MUL, 0, :], W_out0[0:MUL, :]).then_inc(d_up, 16)
        sp.dma_start(W_out_in[0:MUL, 1, :], W_out0[MUL:2 * MUL, :]).then_inc(d_up, 16)
        whole = nodes // P
        sp.dma_start(x_sb[:, 0:whole, :], x[0:whole * P, :].rearrange("(t p) c -> p t c", p=P))\
            .then_inc(d_x, 16)
        if nodes % P:
            sp.dma_start(x_sb[0:nodes % P, whole, :], x[whole * P:nodes, :]).then_inc(d_x, 16)
        sp.wait_ge(s_weights, 1)
        for part in range(3):
            sp.dma_start(bias3[part:part + 1, :, :], bparts[:, part, :])\
                .then_inc(d_bparts, 16)
        for k in range(BESSEL):
            sp.wait_ge(s_emb[k % 2], k // 2 + 1)
            sp.dma_start(emb_dram[:, k::BESSEL, :],
                         emb_k[:, k % 2, :].rearrange("g (h e) -> g h e", h=2))\
                .then_inc(d_emb[k % 2], 16)

        wt_halves = edge_weight.rearrange("(n e) -> n e", e=HALF)

        def load_lengths(h):
            if h.parity:
                return
            g = h.pair_slot
            wait(sp, L0["filt1"], h.upto(3))
            for s in range(2):
                sp.dma_start(basis[s * SPREAD:s * SPREAD + RADIAL, g, :],
                             wt_halves[at(h.number(1, s), 1), :].broadcast_to([RADIAL, HALF]))\
                    .then_inc(L0["r_in"][g], 16)
        sp.wait_ge(s_const, 12)
        for_halves(sp, iterations, load_lengths, 0)

        def load_embedding(h):
            if h.parity:
                return
            g = h.pair_slot
            wait(sp, L1["filt1"], h.pair_upto(2))
            sp.dma_start(emb_in[:, g, :], emb_dram[at(h.pair(), 1), :, :].rearrange("a k e -> (a k) e"))\
                .then_inc(L1["r_in"][g], 16)
        for s in range(2):
            sp.wait_ge(d_emb[s], 16 * BESSEL // 2)
        for_halves(sp, iterations, load_embedding, 0)

        def store_out(u, _):
            if u is None:
                return
            wait(sp, s_ynorm, u.upto())
            rows = out[at(u.tile(P), u.cols), :]
            sp.dma_start(rows.rearrange("(t p) c -> p t c", p=u.rows),
                         unit_out[0:u.rows, u.slot, 0:u.tiles, :]).then_inc(s_out[u.slot], 16)
        for_units(sp, nodes, store_out, 0)
        for s in range(2):
            sp.wait_ge(s_out[s], 16 * (last_unit // 2 + (s <= last_unit % 2)))

    @block.scalar
    def _(act):
        a = nc.scalar
        a.preload_act_table_set("natural_log_exp_and_others")
        act.wait_ge(s_wT, 1)
        a.activation(W_linT[:], bank[6][:, 0:P], ACT.Copy).then_inc(s_wTc, 1)

        def copy_turned(sm):
            def step(u, _):
                if u is None:
                    return
                wait(act, sm["turned"], u.upto())
                wait(act, sm["product"], u.upto(2))
                a.activation(unit_T[:, u.slot, 0:u.cols], bank[u.slot][:, 0:u.cols], ACT.Copy)\
                    .then_inc(sm["copied"], 1)
            for_units(act, nodes, step, 0)

        copy_turned(table0)

        act.wait_ge(s_rclip, 1)
        for k in range(BESSEL):
            if k >= 2:
                act.wait_ge(s_emb[k % 2], k // 2)
                act.wait_ge(d_emb[k % 2], 16 * (k // 2))
            a.activation(emb_k[:, k % 2, :], r_clip, ACT.Square, scale=float(BESSEL - 1),
                         bias=steps8[0:pairs, k:k + 1]).then_inc(s_act, 1)
            act.wait_ge(s_act, k + 1)
            a.activation(emb_k[:, k % 2, :], emb_k[:, k % 2, :], ACT.Exp, scale=-0.5,
                         bias=log_scale[0:pairs, :]).then_inc(s_embsq, 1)
        act.wait_ge(s_norm, 1)
        a.activation(norm, norm, ACT.Sqrt).then_inc(s_norm, 1)
        a.preload_act_table_set("natural_log_exp_and_others")

        def pick(sm, h):
            for s in range(2):
                wait(act, sm["landed"][h.slot + s], h.uses(64, 1))
            cols2 = srcT[:, :, :].rearrange("p a b -> p (a b)")[:, at(h.number(HALF_CHUNKS), 2 * HALF_CHUNKS)]
            a.activation(picks[:, h.pair_slot, :], cols2, ACT.Copy)\
                .then_inc(sm["picked"], 1)

        def make_basis(h):
            g = h.pair_slot
            rows = basis[0:SPREAD + RADIAL, g, :]
            wait(act, L0["r_in"][g], h.uses(32))
            a.activation(rows, rows, ACT.Square, bias=neg_centers[0:SPREAD + RADIAL, :])\
                .then_inc(L0["squared"], 1)
            wait(act, L0["squared"], h.pair_upto())
            delta = np.float32(CUTOFF) / np.float32(RADIAL - 1)
            a.activation(rows, rows, ACT.Exp, scale=-float(1.0 / (2.0 * delta * delta)))\
                .then_inc(L0["basis"], 1)

        def soft_log(sm, parity, n, cols_n, use):
            wait(act, sm["capped"], use)
            tile_ = soft[:, parity, 0:cols_n]
            a.activation(tile_, tile_, ACT.Exp).then_inc(sm[n[0]], 1)
            wait(act, sm[n[0]], use)
            a.activation(tile_, tile_, ACT.Ln, scale=0.5, bias=half_const[:, :])\
                .then_inc(sm[n[1]], 1)

        def layer0(h):
            if h.parity == 0 and h.real():
                pick(L0, h)
                make_basis(h)
            b = h.before(2)
            if b.real():
                soft_log(L0, b.parity, ("exped", "logged"), HALF, b.upto())
        act.wait_ge(s_turned, 2)
        act.wait_ge(s_weights, 1)
        for_halves(act, iterations, layer0, 2)

        def dense_log(u, _):
            if u is not None:
                soft_log(dense0, u.slot, ("soft_e", "soft_l"),
                         u.cols, u.upto())
        for_units(act, nodes, dense_log, 0)

        def root(i):
            act.wait_ge(s_var[i], last_unit + 2)
            a.activation(rstd[:], moments[:, 1, :], ACT.Sqrt, bias=eps[:, :]).then_inc(s_rstd[i], 1)
        root(0)
        copy_turned(table1)

        def layer1(h):
            if h.parity == 0 and h.real():
                pick(L1, h)
                g = h.pair_slot
                wait(act, L1["filt1"], h.pair_upto())
                wait(act, L1["filt2"], h.pair_upto(2))
                a.activation(h1[:, g, :], bank[0][:], ACT.Silu, bias=b0_c).then_inc(L1["act1"], 1)
            if h.parity == 1:
                b = h.before(1)
                if b.real():
                    g = b.pair_slot
                    wait(act, L1["filt2"], b.pair_upto())
                    wait(act, L1["filt"], b.upto(3))
                    a.activation(h2[:, g, :], bank[1][:], ACT.Silu, bias=b1_c)\
                        .then_inc(L1["act2"], 1)
        for_halves(act, iterations, layer1, 0)

        def stage_sums(u, _):
            if u is None:
                return
            wait(act, dense1["second"], u.upto(2))
            n = u.cols
            a.activation(stage[:, u.slot, :, 0:n], sums[:, :, at(u.tile(P), n)], ACT.Copy)\
                .then_inc(dense1["staged"], 1)
        act.wait_ge(L1["added"], halves)
        for_units(act, nodes, stage_sums, 0)
        root(1)

    @block.tensor
    def _(pe):
        t_ = nc.tensor
        pe.wait_ge(s_ident, 1)
        pe.wait_ge(d_wlin, 16)
        t_.transpose(bank[6][:, 0:P], W_lin_sb[:], ident[:]).then_inc(s_wT, 1)

        turns = [0]

        def turn_rows(rows, done=None):
            if turns[0] >= 1:
                pe.wait_ge(s_turned, turns[0])
            for j, r in enumerate(rows):
                last = t_.transpose(quads[7][:, j, 0:pairs], r, ident[0:pairs, 0:pairs])
            last.then_inc(s_turn, 1)
            turns[0] += 1

        def turn_all(tile_rows):
            for j in range(0, pair_chunks, 4):
                turn_rows([tile_rows[:, (j + i) * P:(j + i + 1) * P] for i in range(4)])

        pe.wait_ge(s_dve, 1)
        turn_all(src_f)

        def turn_unit(sm, u):
            if sm is table0:
                wait(pe, sm["loaded"][u.slot], u.uses(16))
            else:
                wait(pe, sm["normed"], u.upto())
            wait(pe, sm["copied"], u.upto(2))
            for t in range(u.tiles):
                last = t_.transpose(bank[u.slot][:, t * P:t * P + u.rows],
                                    unit_in[0:u.rows, u.slot, t, :], ident[0:u.rows, 0:u.rows])
            last.then_inc(sm["turned"], 1)

        def product_unit(sm, u, weight):
            wait(pe, sm["copied"], u.upto())
            wait(pe, sm["ready"], u.upto(2))
            for t in range(u.tiles):
                last = t_.matmul(quads[2 + u.slot][0:u.rows, t, :],
                                 unit_T[:, u.slot, t * P:t * P + u.rows], weight[:],
                                 start=True, stop=True)
            last.then_inc(sm["product"], 1)

        def tables(sm, weight):
            def step(u, before):
                if u is not None:
                    turn_unit(sm, u)
                if before is not None:
                    product_unit(sm, before, weight)
            for_units(pe, nodes, step, 1)

        pe.wait_ge(s_wTc, 1)
        tables(table0, W_linT)

        pe.wait_ge(s_dve, 3)
        turn_all(dst_f[:, :])
        turn_all(rel2)
        pe.wait_ge(s_fits, 1)
        pe.wait_ge(s_const, 2)
        t_.matmul(bank[6][0:1, 0:1], fits_row[:], ones[0:pairs, :], start=True, stop=True)\
            .then_inc(s_flag, 1)
        pe.wait_ge(s_norm, 3)
        for c in range(3):
            turn_all_c = [attr[:, (j * P) * 3 + c:((j + 1) * P - 1) * 3 + c + 1:3]
                          for j in range(pair_chunks)]
            turn_rows(turn_all_c[0:4])
            turn_rows(turn_all_c[4:8])

        def products(out_bank, n_tiles, rows, lhs, weight, which):
            for j in range(n_tiles):
                t_.matmul(out_bank[0:rows, j, :], lhs(j), weight, start=(j == 0), stop=False,
                          skip_group_check=True)
            return t_.matmul(out_bank[0:rows, 0:n_tiles, :], ones_bf[:, 0:rows],
                             bias3[:, which:which + 1, :].broadcast_to([3, n_tiles, P]),
                             start=False, stop=True, skip_group_check=True)

        def window_sums(sm, h, outputs):
            p = h.parity
            wait(pe, sm["msg"], h.upto())
            b = h.before(2)
            wait(pe, sm["added"], b.upto())
            ps = winps[p][:, :].rearrange("p (k n) -> p k n", n=WINDOW)
            for k in range(outputs):
                for j in range(HALF_CHUNKS):
                    last = t_.matmul(ps[:, k, :], msg[:, p, j, k * P:(k + 1) * P],
                                     onehot[:, p, j, :], start=(j == 0),
                                     stop=(j == HALF_CHUNKS - 1))
            last.then_inc(sm["window"], 1)

        def every_window(sm, ev, h, outputs):
            p = h.parity
            first = h.number(all_windows // 2)
            with pe.Fori(1, all_windows // 2 + 1) as i:
                use = pe.snap(i + first)
                wait(pe, sm["msg"], h.upto())
                for q in range(2):
                    ps = winps[q][:, :].rearrange("p (k n) -> p k n", n=WINDOW)
                    pe.wait_ge(ev["onehot"][q], use)
                    pe.wait_ge(ev["added"][q], use)
                    for k in range(outputs):
                        for j in range(HALF_CHUNKS):
                            last = t_.matmul(ps[:, k, :], msg[:, p, j, k * P:(k + 1) * P],
                                             onehot[:, q, j, :], start=(j == 0),
                                             stop=(j == HALF_CHUNKS - 1))
                    last.then_inc(ev["window"][q], 1)

        def hidden0(h):
            p, g = h.parity, h.pair_slot
            b = h.before(SLOTS)
            wait(pe, L0["basis"], h.pair_upto())
            wait(pe, L0["soft"], b.upto())
            rows = slice(p * SPREAD, p * SPREAD + RADIAL)
            t_.matmul(filtA[h.slot][:, :], Wf1_sb[rows, :], basis[rows, g, :], start=True, stop=True)\
                .then_inc(L0["filt1"], 1)

        def filter0(h):
            p = h.parity
            b = h.before(2)
            wait(pe, L0["msg"], b.upto())
            wait(pe, L0["soft"], h.upto())
            products(filtB[p], HALF_CHUNKS, P, lambda j: hid[:, p, j * P:(j + 1) * P], Wf2_sb[:], 0)\
                .then_inc(L0["filt"], 1)

        def hidden1(h):
            g = h.pair_slot
            wait(pe, L1["r_in"][g], h.uses(16))
            b = h.before(2)
            wait(pe, L1["act1"], b.pair_upto())
            t_.matmul(bank[0][:, :], w0_sb[:], emb_in[:, g, :], start=True, stop=True)\
                .then_inc(L1["filt1"], 1)

        def second1(h):
            g = h.pair_slot
            wait(pe, L1["act1"], h.pair_upto())
            b = h.before(2)
            wait(pe, L1["act2"], b.pair_upto())
            t_.matmul(bank[1][:, :], w1_sb[:], h1[:, g, :], start=True, stop=True)\
                .then_inc(L1["filt2"], 1)

        def filter1(h):
            p, g = h.parity, h.pair_slot
            b = h.before(2)
            wait(pe, L1["msg"], b.upto())
            wait(pe, L1["act2"], h.pair_upto())
            rows = slice(p * HIDDEN, (p + 1) * HIDDEN)
            products(filtB[p], HALF_CHUNKS, P, lambda j: h2[rows, g, j * P:(j + 1) * P],
                     w2_sb[rows, :], 2).then_inc(L1["filt"], 1)

        def layer0(h):
            if h.real():
                hidden0(h)
            b = h.before(3)
            if b.real():
                filter0(b)
            b = h.before(5)
            if b.real():
                window_sums(L0, b, 1)

        def layer1(h):
            if h.parity == 0 and h.real():
                hidden1(h)
            b = h.before(1)
            if h.parity == 1 and b.real():
                second1(b)
            b = h.before(3)
            if b.real():
                filter1(b)
            b = h.before(5)
            if b.real():
                window_sums(L1, b, 2)

        def layer0_any(h):
            hidden0(h)
            filter0(h)
            every_window(L0, every[0], h, 1)

        def layer1_any(h):
            if h.parity == 0:
                hidden1(h)
                second1(h)
            filter1(h)
            every_window(L1, every[1], h, 2)

        def tables_read(sm):
            pe.wait_ge(sm["ready"], last_unit + 1)
        tables_read(table0)
        pe.wait_ge(d_weights, 16 * 5)
        pe.wait_ge(d_bparts, 48)
        pe.wait_ge(s_turned, 12)
        pe.wait_ge(s_flag, 2)
        flag = pe.value_load(sorted_flag[0:1, 0:1], min_val=0, max_val=1)
        with pe.If(flag):
            for_halves(pe, iterations, layer0, 5)
        with pe.Else():
            for_halves(pe, iterations, layer0_any, 0)

        def dense_first(u):
            n = u.cols
            wait(pe, dense0["hidden"], u.upto(2))
            t_.matmul(filtA[u.slot][:, 0:n], Wm1_sb[:], sums[:, 0, at(u.tile(P), n)],
                      start=True, stop=True).then_inc(dense0["first"], 1)

        def dense_second(u):
            wait(pe, dense0["added"], u.upto(2))
            wait(pe, dense0["hidden"], u.upto())
            products(filtB[u.slot], u.tiles, u.rows,
                     lambda t: hid[:, u.slot, t * P:t * P + u.rows], Wm2_sb[:], 1)\
                .then_inc(dense0["second"], 1)

        def dense(u, before):
            if u is not None:
                dense_first(u)
            if before is not None:
                dense_second(before)
        pe.wait_ge(L0["added"], halves)
        for_units(pe, nodes, dense, 1)
        pe.wait_ge(d_up, 16 * 18)
        tables(table1, W_up_sb)
        tables_read(table1)
        flag = pe.value_load(sorted_flag[0:1, 0:1], min_val=0, max_val=1)
        with pe.If(flag):
            for_halves(pe, iterations, layer1, 5)
        with pe.Else():
            for_halves(pe, iterations, layer1_any, 0)

        def outputs(u, _):
            if u is None:
                return
            wait(pe, dense1["staged"], u.upto())
            wait(pe, dense1["added"], u.upto(2))
            for t in range(u.tiles):
                for k, w in enumerate((W_outA, W_outB)):
                    last = t_.matmul(filtB[u.slot][0:u.rows, t, :],
                                     stage[:, u.slot, k, t * P:t * P + u.rows], w[:],
                                     start=(k == 0), stop=(k == 1))
            last.then_inc(dense1["second"], 1)
        for_units(pe, nodes, outputs, 0)

    @block.vector
    def _(dve):
        v = nc.vector
        steps = [0]

        def then(ins):
            steps[0] += 1
            ins.then_inc(s_own, 1)
            dve.wait_ge(s_own, steps[0])

        dve.wait_ge(d_rows[0], 16)
        v.tensor_copy(src_f, src_i[:]).then_inc(s_dve, 1)

        turned = [0]

        def copy_turn(tile_T, j):
            turned[0] += 1
            dve.wait_ge(s_turn, turned[0])
            v.tensor_copy(tile_T[:, :, j:j + 4].rearrange("p g j -> p j g"),
                          quads[7][:, :, 0:pairs]).then_inc(s_turned, 1)

        copy_turn(srcT, 0)
        copy_turn(srcT, 4)
        for w_sb in (w0_sb, w1_sb, W_up_sb, W_outA, W_outB):
            last = v.memset(w_sb[:], 0.0)
        last.then_inc(s_blocks, 1)

        def copy_product(sm):
            def step(u, _):
                if u is None:
                    return
                wait(dve, sm["product"], u.upto())
                wait(dve, sm["stored"][u.slot], u.uses(16, 1))
                scale = 1.0 if sm is table0 else 1.0 / math.sqrt(MUL)
                v.tensor_scalar(unit_out[0:u.rows, u.slot, 0:u.tiles, :],
                                quads[2 + u.slot][0:u.rows, 0:u.tiles, :], scale, None, ALU.mult)\
                    .then_inc(sm["ready"], 1)
            return step

        for_units(dve, nodes, copy_product(table0), 0)

        dve.wait_ge(d_rows[1], 16)
        v.tensor_copy(dst_f[:], dst_i[:]).then_inc(s_dve, 1)
        dve.wait_ge(s_dve, 2)
        d3 = dst_f[:, :].rearrange("g (a b) -> g a b", b=HALF)
        v.tensor_tensor(rel_f, d3, d3[:, :, 0:1].broadcast_to([pairs, 2, HALF]),
                        ALU.subtract).then_inc(s_dve, 1)
        dve.wait_ge(s_dve, 3)
        then(v.tensor_scalar(fits, rel2, 0.0, None, ALU.is_ge))
        then(v.scalar_tensor_tensor(out=fits, in0=rel2, scalar=float(WINDOW), in1=fits,
                                    op0=ALU.is_lt, op1=ALU.mult))
        then(v.scalar_tensor_tensor(out=fits, in0=dst_f[:], scalar=float(nodes), in1=fits,
                                    op0=ALU.is_ge, op1=ALU.max))
        v.tensor_reduce(fits_row[:], fits, AXES.X, ALU.min).then_inc(s_fits, 1)
        for tile_T in (dstT, relT):
            copy_turn(tile_T, 0)
            copy_turn(tile_T, 4)
        dve.wait_ge(s_flag, 1)
        v.tensor_scalar(sorted_flag[:], bank[6][0:1, 0:1], pairs - 0.5, None, ALU.is_ge)\
            .then_inc(s_flag, 1)

        dve.wait_ge(s_const, 12)
        delta = np.float32(CUTOFF) / np.float32(RADIAL - 1)
        then(v.tensor_scalar(neg_centers[:], neg_centers[:], -float(delta), None, ALU.mult))
        then(v.tensor_scalar(steps8[:], steps8[:], -1.0, None, ALU.mult))
        dve.wait_ge(d_bias, 16 * 9)
        then(v.tensor_scalar(bf1_s, bf1_c, -math.log(2.0), None, ALU.add))
        then(v.tensor_scalar(bm1_s, bm1_c, -math.log(2.0), None, ALU.add))
        b_all = brow[:, :, :].rearrange("a b c -> a (b c)")
        r_all = brest[:, :, :].rearrange("a b c -> a (b c)")
        then(v.tensor_copy(bparts[:, 0, :], b_all))
        then(v.tensor_tensor(r_all, b_all, bparts[:, 0, :], ALU.subtract))
        then(v.tensor_copy(bparts[:, 1, :], r_all))
        then(v.tensor_tensor(r_all, r_all, bparts[:, 1, :], ALU.subtract))
        then(v.tensor_copy(bparts[:, 2, :], r_all))
        dve.wait_ge(d_rows[2], 16)
        v.tensor_scalar(r_mask, wt_rows[:], 1.0, None, ALU.is_le)
        v.tensor_scalar(r_clip, wt_rows[:], 0.0, 1.0, ALU.max, ALU.min).then_inc(s_rclip, 1)
        dve.wait_ge(d_rows[3], 16)
        then(v.tensor_tensor(attr_sq, attr, attr, ALU.mult))
        v.tensor_reduce(norm, attr_sq.rearrange("g (e c) -> g e c", c=3), AXES.X, ALU.add)\
            .then_inc(s_norm, 1)
        dve.wait_ge(d_up, 16 * 18)
        out_scale = 1.0 / (math.sqrt(2 * MUL) * AVG_DEGREE)
        root3 = math.sqrt(3.0)
        for k, w_sb in enumerate((W_outA, W_outB)):
            v.tensor_scalar(w_sb[0:MUL, 0:MUL], W_out_in[0:MUL, k, :], out_scale, None, ALU.mult)
            for c in range(3):
                cs = slice(MUL * (c + 1), MUL * (c + 2))
                last = v.tensor_scalar(w_sb[cs, MUL + c:P:3], W_out_in[cs, k, :],
                                       out_scale * (root3 if k else 1.0), None, ALU.mult)
        last.then_inc(s_weights, 1)
        for k in range(BESSEL):
            dve.wait_ge(s_embsq, k + 1)
            v.tensor_tensor(emb_k[:, k % 2, :], emb_k[:, k % 2, :], r_mask, ALU.mult)\
                .then_inc(s_emb[k % 2], 1)
        dve.wait_ge(s_norm, 2)
        then(v.tensor_scalar(norm, norm, 1e-12, None, ALU.add))
        then(v.reciprocal(norm, norm))
        v.tensor_tensor(attr.rearrange("g (e c) -> g e c", c=3),
                        attr.rearrange("g (e c) -> g e c", c=3),
                        norm.rearrange("g (e c) -> g e c", c=1)
                        .broadcast_to([pairs, PAIR, 3]), ALU.mult).then_inc(s_norm, 1)
        for c in range(3):
            copy_turn(dirT[:, :, :, c], 0)
            copy_turn(dirT[:, :, :, c], 4)

        def one_hots(h, sm):
            p = h.parity
            b = h.before(2)
            wait(dve, sm["window"], b.upto())
            v.tensor_tensor(onehot[:, p],
                            by_chunk(relT, h).rearrange("p (j a) -> p j a", a=1)
                            .broadcast_to([P, HALF_CHUNKS, WINDOW]),
                            iota[:, :].rearrange("p (a n) -> p a n", a=1)
                            .broadcast_to([P, HALF_CHUNKS, WINDOW]), ALU.is_equal)

        def add_window(sm, h, outputs, base):
            ps = winps[h.parity][:, :].rearrange("p (k n) -> p k n", n=WINDOW)
            wait(dve, sm["window"], h.upto())
            b = h.before(1)
            wait(dve, sm["added"], b.upto())
            here = sums[:, 0:outputs, at(base, WINDOW)]
            v.tensor_tensor(here, here, ps[:, 0:outputs, :], ALU.add).then_inc(sm["added"], 1)

        def cap0(h):
            p = h.parity
            b = h.before(2)
            wait(dve, L0["soft"], b.upto())
            wait(dve, L0["filt1"], h.upto())
            v.tensor_scalar(soft[:, p, :], filtA[h.slot][:, :], bf1_c, EXP_CAP, ALU.add, ALU.min)\
                .then_inc(L0["capped"], 1)

        def soft0(h):
            p = h.parity
            b = h.before(2)
            wait(dve, L0["filt"], b.upto())
            wait(dve, L0["logged"], h.upto())
            v.scalar_tensor_tensor(out=hid[:, p, :], in0=filtA[h.slot][:, :], scalar=bf1_s,
                                   in1=soft[:, p, :], op0=ALU.add, op1=ALU.max)\
                .then_inc(L0["soft"], 1)

        def msg0(h):
            p = h.parity
            wait(dve, L0["filt"], h.upto())
            wait(dve, L0["landed"][h.slot], h.uses(64))
            b = h.before(2)
            wait(dve, L0["window"], b.upto())
            v.tensor_tensor(msg[:, p, :, 0:P], filtB[p], sent[:, h.slot], ALU.mult)\
                .then_inc(L0["msg"], 1)

        def msg1(h):
            p = h.parity
            filt = filtB[p].rearrange("p j (i m) -> p j i m", m=MUL)
            rows = sent[:, h.slot]
            vec = rows[:, :, MUL:].rearrange("p j (c m) -> p j c m", m=MUL)
            cube = [P, HALF_CHUNKS, 3, MUL]
            dirs = dirT[:, :, :, :].rearrange("p a b c -> p (a b) c")[:, at(h.number(HALF_CHUNKS), HALF_CHUNKS), :]\
                .rearrange("p j (c m) -> p j c m", m=1).broadcast_to(cube)
            wait(dve, L1["landed"][h.slot], h.uses(64))
            v.tensor_tensor(dots[:, p], vec, dirs, ALU.mult).then_inc(L1["dots"], 1)
            wait(dve, L1["filt"], h.upto())
            b = h.before(2)
            wait(dve, L1["window"], b.upto())
            scaled = msg[:, p, :, :].rearrange("p j (q m) -> p j q m", m=MUL)[:, :, 0:9:8, :]
            v.tensor_tensor(scaled, filt[:, :, 0:2, :],
                            rows[:, :, 0:MUL].rearrange("p j (a m) -> p j a m", a=1)
                            .broadcast_to([P, HALF_CHUNKS, 2, MUL]), ALU.mult)\
                .then_inc(L1["scaled"], 1)
            wait(dve, L1["dots"], h.upto())
            v.tensor_reduce(dot[:, p], dots[:, p].rearrange("p j c m -> p j m c"), AXES.X, ALU.add)\
                .then_inc(L1["dot"], 1)
            v.tensor_tensor(msg[:, p, :, MUL:P].rearrange("p j (c m) -> p j c m", m=MUL), vec,
                            filt[:, :, 2:3, :].broadcast_to(cube), ALU.mult)
            wait(dve, L1["scaled"], h.upto())
            v.tensor_tensor(msg[:, p, :, P + MUL:2 * P].rearrange("p j (c m) -> p j c m", m=MUL),
                            msg[:, p, :, 2 * P:].rearrange("p j (a m) -> p j a m", a=1)
                            .broadcast_to(cube), dirs, ALU.mult)
            wait(dve, L1["dot"], h.upto())
            v.tensor_tensor(msg[:, p, :, P:P + MUL], filt[:, :, 3, :], dot[:, p], ALU.mult)\
                .then_inc(L1["msg"], 1)

        def loop_layer(step, lag):
            def load_bases(first, n):
                if n <= 0:
                    return []
                _, values = nc.values_load_multi_w_load_instructions(
                    bases[0:1, at(first, n)], engines=[mybir.EngineType.DVE], min_val=0,
                    max_val=width - WINDOW, skip_runtime_bounds_check_because="receivers are nodes")
                return values
            count = iterations * SLOTS
            peeled = min(2, iterations)

            def steps_of(halves_, first, values):
                for i, h in enumerate(halves_):
                    step(h, values[i + first] if i + first >= 0 else None)

            for it in range(peeled):
                first = it * SLOTS - lag
                values = load_bases(max(first, 0), first + SLOTS - max(first, 0))
                steps_of([Half(it * SLOTS + s, count) for s in range(SLOTS)], min(first, 0), values)
            if iterations > peeled:
                with dve.Fori(peeled, iterations) as it:
                    counter = Counter(dve, it)
                    values = load_bases(counter.value(SLOTS, -lag), SLOTS)
                    steps_of([Half(s, count, counter) for s in range(SLOTS)], 0, values)
            values = load_bases(count - lag, lag)
            steps_of([Half(n, count) for n in range(count, count + lag)], 0, values)

        def layer0(h, base):
            b1, b2, b4, b6 = (h.before(i) for i in (1, 2, 4, 6))
            if b1.real():
                cap0(b1)
            if b4.real():
                one_hots(b4, L0)
                msg0(b4)
            if b6.real():
                add_window(L0, b6, 1, base)
            if b2.real():
                soft0(b2)

        def layer1(h, base):
            b4, b6 = h.before(4), h.before(6)
            if b6.real():
                add_window(L1, b6, 2, base)
            if b4.real():
                one_hots(b4, L1)
                msg1(b4)

        def every_window(sm, ev, h, outputs):
            first = h.number(all_windows // 2)
            targets = by_chunk(dstT, h)

            def hots(i, q):
                lo = i * (2 * WINDOW) + (q - 2) * WINDOW
                v.tensor_tensor(onehot[:, q],
                                targets.rearrange("p (j a) -> p j a", a=1)
                                .broadcast_to([P, HALF_CHUNKS, WINDOW]),
                                windows_iota[:, bass.ds(lo, WINDOW)]
                                .rearrange("p (a n) -> p a n", a=1)
                                .broadcast_to([P, HALF_CHUNKS, WINDOW]), ALU.is_equal)\
                    .then_inc(ev["onehot"][q], 1)

            with dve.Fori(1, all_windows // 2 + 1) as i:
                use = dve.snap(i + first)
                more = dve.snap(use + 1)
                for q in range(2):
                    dve.wait_ge(ev["window"][q], use)
                    hots(i, q)
                for q in range(2):
                    ps = winps[q][:, :].rearrange("p (k n) -> p k n", n=WINDOW)
                    here = sums[:, 0:outputs, bass.ds(i * (2 * WINDOW) + (q - 2) * WINDOW, WINDOW)]
                    dve.wait_ge(ev["window"][q], more)
                    v.tensor_tensor(here, here, ps[:, 0:outputs, :], ALU.add)\
                        .then_inc(ev["added"][q], 1)
            dve.sem_inc(sm["window"], 1)
            dve.wait_ge(ev["added"][1], h.number(all_windows // 2, all_windows // 2 + 1))
            dve.sem_inc(sm["added"], 1)

        def layer0_any(h):
            cap0(h)
            soft0(h)
            msg0(h)
            every_window(L0, every[0], h, 1)

        def layer1_any(h):
            msg1(h)
            every_window(L1, every[1], h, 2)

        dve.wait_ge(d_bases, 16)
        dve.wait_ge(s_flag, 2)
        flag = dve.value_load(sorted_flag[0:1, 0:1], min_val=0, max_val=1)
        with dve.If(flag):
            loop_layer(layer0, 6)
        with dve.Else():
            for q in range(2):
                dve.sem_inc(every[0]["window"][q], 1)
                dve.sem_inc(every[0]["added"][q], 1)
            for_halves(dve, iterations, layer0_any, 0)

        def norm_stats(sm, u, moved):
            rows = slice(0, u.rows)
            here = x_sb[rows, at(u.tile(), u.tiles), :]
            v.tensor_tensor(here, filtB[u.slot][rows, 0:u.tiles, :], here, ALU.add)\
                .then_inc(sm["added"], 1)
            wait(dve, sm["added"], u.upto())
            dve.sem_inc(s_measuring, 1)
            for t in range(u.tiles):
                last = v.bn_stats(stats[rows, u.slot, t, :],
                                  x_sb[rows, at(u.tile(1, t), 1), :].rearrange("p a c -> p (a c)"))
            last.then_inc(sm["stats"], 1)
            wait(dve, sm["stats"], u.upto())
            v.tensor_scalar(all_stats[rows, at(u.tile(), u.tiles), :], stats[rows, u.slot, 0:u.tiles],
                            1.0, None, ALU.mult).then_inc(moved, 1)

        def dense(u, before):
            if u is not None:
                n = u.cols
                wait(dve, dense0["first"], u.upto())
                v.tensor_scalar(soft[:, u.slot, 0:n], filtA[u.slot][:, 0:n], bm1_c, EXP_CAP,
                                ALU.add, ALU.min).then_inc(dense0["capped"], 1)
            if before is not None:
                wait(dve, dense0["second"], before.upto())
                norm_stats(dense0, before, s_var[0])
            if u is not None:
                wait(dve, dense0["soft_l"], u.upto())
                wait(dve, dense0["second"], u.upto(2))
                v.scalar_tensor_tensor(out=hid[:, u.slot, 0:n], in0=filtA[u.slot][:, 0:n],
                                       scalar=bm1_s, in1=soft[:, u.slot, 0:n], op0=ALU.add,
                                       op1=ALU.max).then_inc(dense0["hidden"], 1)
        dve.wait_ge(d_x, 16 * (1 + bool(nodes % P)))
        then(v.memset(all_stats[:], 0.0))
        for_units(dve, nodes, dense, 1)

        def invert(i):
            mean, var, diff = (moments[:, m, :] for m in range(3))
            even, odd = all_stats[:, :, 1], all_stats[:, :, 4]
            dve.wait_ge(s_var[i], last_unit + 1)
            then(v.tensor_tensor(mean, even, odd, ALU.add))
            then(v.tensor_scalar(mean, mean, 0.5, None, ALU.mult))
            then(v.tensor_tensor(diff, even, mean, ALU.subtract))
            then(v.tensor_tensor(diff, diff, diff, ALU.mult))
            then(v.tensor_tensor(var, all_stats[:, :, 2], all_stats[:, :, 5], ALU.add))
            v.scalar_tensor_tensor(out=var, in0=var, scalar=1.0 / P, in1=diff, op0=ALU.mult,
                                   op1=ALU.add).then_inc(s_var[i], 1)
            dve.wait_ge(s_rstd[i], 1)
            v.reciprocal(rstd[:], rstd[:]).then_inc(s_rstd[i], 1)
            dve.wait_ge(s_rstd[i], 2)

        def normalise(u, target, t):
            rows = slice(0, u.rows)
            col = u.tile(1, t)
            return v.tensor_scalar(target, x_sb[rows, at(col, 1), :].rearrange("p a c -> p (a c)"),
                                   moments[rows, 0, at(col, 1)],
                                   rstd[rows, at(col, 1)], ALU.subtract, ALU.mult)

        invert(0)

        def norm_and_table(u, before):
            if u is not None:
                rows = slice(0, u.rows)
                wait(dve, table1["turned"], u.upto(2))
                for t in range(u.tiles):
                    last = normalise(u, unit_in[rows, u.slot, t, :], t)
                last.then_inc(table1["normed"], 1)
                wait(dve, table1["normed"], u.upto())
                v.tensor_scalar(x_sb[rows, at(u.tile(), u.tiles), :],
                                unit_in[rows, u.slot, 0:u.tiles, :], 1.0, None, ALU.mult)
            if before is not None:
                copy_product(table1)(before, None)
        for_units(dve, nodes, norm_and_table, 1)

        dve.wait_ge(s_zeroed, 1)
        flag = dve.value_load(sorted_flag[0:1, 0:1], min_val=0, max_val=1)
        with dve.If(flag):
            loop_layer(layer1, 6)
        with dve.Else():
            for q in range(2):
                dve.sem_inc(every[1]["window"][q], 1)
                dve.sem_inc(every[1]["added"][q], 1)
            for_halves(dve, iterations, layer1_any, 0)

        def residual1(u, _):
            if u is not None:
                wait(dve, dense1["second"], u.upto())
                norm_stats(dense1, u, s_var[1])
        for_units(dve, nodes, residual1, 0)
        invert(1)

        def finish(u, _):
            if u is not None:
                rows = slice(0, u.rows)
                wait(dve, s_out[u.slot], u.uses(16, 1))
                for t in range(u.tiles):
                    last = normalise(u, unit_out[rows, u.slot, t, :], t)
                last.then_inc(s_ynorm, 1)
        for_units(dve, nodes, finish, 0)


def kernel(**inputs):
    import concourse.bacc as bacc
    from concourse.bass_utils import run_bass_kernel_spmd

    x = np.ascontiguousarray(inputs["x"])
    nodes = x.shape[0]
    edges = inputs["src"].shape[0]
    more = padded_edges(edges) - edges
    arrays = {"x": x}
    for name, fill in (("src", 0), ("dst", pad_receiver(nodes)), ("edge_attr_3", 0),
                       ("edge_weight", 0)):
        a = np.asarray(inputs[name])
        tail = np.full((more,) + a.shape[1:], fill, a.dtype)
        arrays[name] = np.ascontiguousarray(np.concatenate([a, tail]))
    for name in ("L0_gnn_W_lin", "L0_gnn_Wf1", "L0_gnn_bf1", "L0_gnn_Wf2", "L0_gnn_bf2",
                 "L0_gnn_Wm1", "L0_gnn_bm1", "L0_gnn_Wm2", "L0_gnn_bm2", "L1_gnn_W_up0",
                 "L1_gnn_W_up1", "L1_gnn_mlp_w0", "L1_gnn_mlp_b0", "L1_gnn_mlp_w1",
                 "L1_gnn_mlp_b1", "L1_gnn_mlp_w2", "L1_gnn_mlp_b2", "L1_gnn_W_out0",
                 "L1_gnn_W_out1"):
        arrays[name] = np.ascontiguousarray(inputs[name])
    nc = bacc.Bacc("TRN2", target_bir_lowering=False, num_devices=1)
    args = [nc.dram_tensor(f"in_{k}", a.shape, mybir.dt.from_np(a.dtype), kind="ExternalInput").ap()
            for k, a in arrays.items()]
    args.append(nc.dram_tensor("out", x.shape, F32, kind="ExternalOutput").ap())
    with ExitStack() as ctx:
        build(nc, *args, ctx)
    r = run_bass_kernel_spmd(nc, [{f"in_{k}": a for k, a in arrays.items()}], core_ids=[0])
    return r.results[0]["out"]
```

```python
from contextlib import ExitStack
import math

import numpy as np
import concourse.bass as bass
from concourse import mybir

F32 = mybir.dt.float32
BF16 = mybir.dt.bfloat16
I32 = mybir.dt.int32
I16 = mybir.dt.int16
ALU = mybir.AluOpType
ACT = mybir.ActivationFunctionType
AXES = mybir.AxisListType

P = 128
HALF_CHUNKS = 4
HALF = HALF_CHUNKS * P
SLOTS = 4
PAIR = 2 * HALF
WINDOW = 128
UNIT_TILES = 4
LN_EPS = 1e-5
EXP_CAP = 40.0

RADIAL, CUTOFF = 50, 5.0
BESSEL = 8
MUL = 32
HIDDEN = 64
AVG_DEGREE = 16.0
SPREAD = 64
ROWS = RADIAL + BESSEL
FAR = 64.0


def padded_edges(edges):
    return -(-edges // (SLOTS * HALF)) * SLOTS * HALF


def pad_receiver(nodes):
    return -(-nodes // P) * P


class Counter:

    def __init__(self, eng=None, it=0):
        self.eng, self.it, self.known = eng, it, {}

    def value(self, scale, offset):
        if self.eng is None:
            return offset
        if (scale, offset) not in self.known:
            self.known[scale, offset] = self.eng.snap(self.it * scale + offset)
        return self.known[scale, offset]


class Half:

    def __init__(self, rel, count, counter=None):
        self.rel, self.count, self.counter = rel, count, counter or Counter()
        self.slot, self.pair_slot, self.parity = rel % SLOTS, rel // 2 % 2, rel % 2

    def real(self):
        return self.counter.eng is not None or 0 <= self.rel < self.count

    def before(self, k):
        return Half(self.rel - k, self.count, self.counter)

    def number(self, scale=1, plus=0):
        return self.counter.value(SLOTS * scale, self.rel * scale + plus)

    def upto(self, back=0):
        return self.counter.value(SLOTS, self.rel + 1 - back)

    def pair_upto(self, back=0):
        return self.counter.value(SLOTS // 2, self.rel // 2 + 1 - back)

    def pair(self):
        return self.counter.value(SLOTS // 2, self.rel // 2)

    def uses(self, scale, back=0):
        return self.counter.value(scale, (self.rel // SLOTS + 1 - back) * scale)


def wait(eng, sem, value):
    if not isinstance(value, int) or value > 0:
        eng.wait_ge(sem, value)


def for_halves(eng, iterations, step, behind):
    count = iterations * SLOTS
    peeled = min(2, iterations)
    for n in range(peeled * SLOTS):
        step(Half(n, count))
    if iterations > peeled:
        with eng.Fori(peeled, iterations) as it:
            counter = Counter(eng, it)
            for s in range(SLOTS):
                step(Half(s, count, counter))
    for n in range(count, count + behind):
        step(Half(n, count))


class Unit:

    def __init__(self, rel, tiles, rows, counter=None):
        self.rel, self.tiles, self.rows, self.counter = rel, tiles, rows, counter or Counter()
        self.slot = rel % 2
        self.cols = tiles * P if rows == P else rows

    def upto(self, back=0):
        return self.counter.value(2, self.rel + 1 - back)

    def uses(self, scale, back=0):
        return self.counter.value(scale, (self.rel // 2 + 1 - back) * scale)

    def tile(self, scale=1, plus=0):
        return self.counter.value(2 * UNIT_TILES * scale, self.rel * UNIT_TILES * scale + plus)


def fixed_unit(number, nodes):
    if number < 0 or number * UNIT_TILES * P >= nodes:
        return None
    left = nodes - number * UNIT_TILES * P
    tiles = min(UNIT_TILES, -(-left // P))
    assert tiles == 1 or left >= tiles * P
    return Unit(number, tiles, min(P, left))


def for_units(eng, nodes, step, behind):
    whole = nodes // (UNIT_TILES * P) // 2
    units = -(-nodes // (UNIT_TILES * P))
    peeled = min(2, whole)
    for n in range(2 * peeled):
        step(lambda k: fixed_unit(n - k, nodes))
    if whole > peeled:
        with eng.Fori(peeled, whole) as it:
            counter = Counter(eng, it)
            for s in range(2):
                step(lambda k: Unit(s - k, UNIT_TILES, P, counter))
    for n in range(2 * whole, units + behind):
        step(lambda k: fixed_unit(n - k, nodes))


def each_unit(eng, nodes, step):
    def own(back):
        if back(0) is not None:
            step(back(0))
    for_units(eng, nodes, own, 0)


def build(nc, x, src, dst, edge_attr, edge_weight, W_lin, Wf1, bf1, Wf2, bf2, Wm1, bm1, Wm2, bm2,
          W_up0, W_up1, mlp_w0, mlp_b0, mlp_w1, mlp_b1, mlp_w2, mlp_b2, W_out0, W_out1, out, ctx):
    nodes, chans = x.shape
    edges = src.shape[0]
    iterations = edges // (SLOTS * HALF)
    halves = iterations * SLOTS
    chunks = halves * HALF_CHUNKS
    pairs = halves // 2
    pair_chunks = PAIR // P
    tiles = -(-nodes // P)
    last_unit = -(-nodes // (UNIT_TILES * P)) - 1
    width = tiles * P + P
    all_windows = width // WINDOW
    assert chans == P and pairs <= P and all_windows % 2 == 0

    def sb(name, shape, dt=F32):
        return ctx.enter_context(nc.sbuf_tensor(name, shape, dt))

    def sem(name):
        return ctx.enter_context(nc.semaphore(name))

    def sems(name, n):
        return [sem(f"{name}{i}") for i in range(n)]

    h_dram = nc.dram_tensor("h_table", (nodes, P), F32).ap()
    v_dram = nc.dram_tensor("up_table", (nodes, P), F32).ap()
    near_dram = nc.dram_tensor("near_lengths", (halves, HALF), F32).ap()
    emb_dram = nc.dram_tensor("radial_embedding", (pairs, 2 * BESSEL, HALF), F32).ap()

    x_sb = sb("x_sb", [P, tiles, P])
    sums = sb("sums", [P, 2, width])
    scratch = sums[:, 1, :]
    windows_iota = sb("windows_iota", [P, all_windows * WINDOW], I16)
    iota = sb("iota", [P, WINDOW])
    ident = sb("ident", [P, P])
    ones = sb("ones", [P, 1])
    ones_bf = sb("ones_bf", [3, P], BF16)
    eps = sb("eps", [P, 1])
    exp_scale = sb("exp_scale", [P, 1])
    exp_bias = sb("exp_bias", [P, 1])
    is_radial, is_bessel = sb("is_radial", [P, 1]), sb("is_bessel", [P, 1])
    half_const = sb("half_const", [P, 1])

    W_lin_sb, W_linT = sb("W_lin_sb", [P, P]), sb("W_linT", [P, P])
    Wf1_sb = sb("Wf1_sb", [SPREAD + RADIAL, P])
    Wf2_sb, Wm1_sb, Wm2_sb = (sb(n, [P, P]) for n in ("Wf2_sb", "Wm1_sb", "Wm2_sb"))
    W_up_sb, W_outA, W_outB = (sb(n, [P, P]) for n in ("W_up_sb", "W_outA", "W_outB"))
    W_out_in = sb("W_out_in", [P, 2, MUL])
    w0_sb = sb("w0_sb", [2 * BESSEL, P])
    w1_sb = sb("w1_sb", [P, P])
    w2_sb = sb("w2_sb", [P, P])
    cols = sb("cols", [P, 6])
    bf1_c, bf1_s, bm1_c, bm1_s, b0_c, b1_c = (cols[:, i:i + 1] for i in range(6))
    brow = sb("brow", [1, 3, P])
    brest = sb("brest", [1, 3, P])
    bparts = sb("bparts", [1, 3, 3 * P], BF16)
    bias3 = sb("bias3", [3, 3, P], BF16)
    neg_centers = sb("neg_centers", [P, 1])

    dst_f = sb("dst_f", [pairs, PAIR])
    fits_row = sb("fits_row", [pairs, 1])
    sorted_flag = sb("sorted_flag", [1, 1], I32)
    srcT = sb("srcT", [P, pairs, pair_chunks])
    dstT = sb("dstT", [P, pairs, pair_chunks])
    relT = sb("relT", [P, pairs, pair_chunks])
    dirT = sb("dirT", [P, pairs, pair_chunks, 3])
    bases = sb("bases", [1, halves], I32)
    wt_rows = sb("wt_rows", [pairs, PAIR])
    all_chunks = pairs * pair_chunks
    attr = scratch[0:pairs, 0:3 * PAIR]
    squares = scratch[:, 3 * PAIR:3 * PAIR + 3 * all_chunks]
    norm = scratch[:, 3 * PAIR + 3 * all_chunks:3 * PAIR + 4 * all_chunks]
    assert 3 * PAIR + 4 * all_chunks <= width

    sent = sb("sent", [P, SLOTS, HALF_CHUNKS, P])
    picks = sb("picks", [P, 2, 2 * HALF_CHUNKS], I32)
    basis = sb("basis", [P, 2, HALF])
    soft = sb("soft", [P, 2, HALF])
    hid = sb("hid", [P, 2, HALF])
    src_i = sb("src_i", [pairs, PAIR], I32)
    dst_i = sb("dst_i", [pairs, PAIR], I32)
    msg = sb("msg", [P, 2, HALF_CHUNKS, 2 * P + MUL])
    dots = sb("dots", [P, 2, HALF_CHUNKS, 3, MUL])
    dot = sb("dot", [P, 2, HALF_CHUNKS, MUL])
    onehot = sb("onehot", [P, 2, HALF_CHUNKS, WINDOW])
    emb_in = sb("emb_in", [2 * BESSEL, 2, HALF])
    h1 = sb("h1", [P, 2, HALF])
    h2 = sb("h2", [P, 2, HALF])
    msg_flat = msg[:, :, :, :].rearrange("p a b c -> p (a b c)")
    src_f, rel2 = msg_flat[0:pairs, 0:PAIR], msg_flat[0:pairs, PAIR:2 * PAIR]
    rel_f = rel2.rearrange("g (a b) -> g a b", b=HALF)

    def rows_of(like):
        return like[0:pairs, :, :].rearrange("p a b -> p (a b)")
    fits, beyond = rows_of(h1), rows_of(h2)

    unit_in = sb("unit_in", [P, 2, UNIT_TILES, P])
    unit_T = sb("unit_T", [P, 2, UNIT_TILES * P])
    unit_out = sb("unit_out", [P, 2, UNIT_TILES, P])
    stage = sent[:, :, :, :].rearrange("p (s k) j c -> p s k (j c)", k=2)
    stats = sb("stats", [P, 2, UNIT_TILES, 6])
    all_stats = sb("all_stats", [P, tiles, 6])
    moments = sb("moments", [P, 3, tiles])
    rstd = sb("rstd", [P, tiles])

    bank = [ctx.enter_context(nc.psum_tensor(f"bank{i}", [P, HALF], F32)) for i in range(8)]
    quads = [b[:, :].rearrange("p (j c) -> p j c", j=4) for b in bank]
    filtA = [bank[i] for i in (0, 1, 6, 7)]
    filtB = quads[2:4]
    winps = bank[4:6]

    s_const = sem("s_const")
    s_ident = sem("s_ident")
    s_measuring = sem("s_measuring")
    s_gathering = sem("s_gathering")
    s_pool = sem("s_pool")
    d_rows = sems("d_rows", 4)
    s_near, d_near = sem("s_near"), sem("d_near")
    d_wlin, d_weights, d_bias = sem("d_wlin"), sem("d_weights"), sem("d_bias")
    d_x, d_bases, d_up = sem("d_x"), sem("d_bases"), sem("d_up")
    d_bparts = sem("d_bparts")
    s_blocks = sem("s_blocks")
    s_dve = sem("s_dve")
    s_own = sem("s_own")
    s_wT, s_wTc = sem("s_wT"), sem("s_wTc")
    s_turn, s_turned = sem("s_turn"), sem("s_turned")
    s_act = sem("s_act")
    s_weights = sem("s_weights")
    s_flag, s_fits = sem("s_flag"), sem("s_fits")
    d_emb = sems("d_emb", 2)
    s_norm = sem("s_norm")

    def unit_sems(phase):
        by_dma = {k: sems(f"{phase}_{k}", 2) for k in ("loaded", "stored")}
        return by_dma | {k: sem(f"{phase}_{k}") for k in
                         ("normed", "turned", "copied", "product", "ready")}

    def dense_sems(phase):
        return {k: sem(f"{phase}_{k}") for k in
                ("staged", "first", "capped", "soft_e", "soft_l", "hidden", "second", "added", "stats")}

    table0, table1 = unit_sems("tab0"), unit_sems("tab1")
    dense0, dense1 = dense_sems("den0"), dense_sems("den1")
    s_var, s_rstd = sems("s_var", 2), sems("s_rstd", 2)
    s_out = sems("s_out", 2)
    s_ynorm = sem("s_ynorm")
    s_zeroed = sem("s_zeroed")

    def edge_sems(layer):
        by_dma = {"r_in": sems(f"L{layer}_r_in", 2), "landed": sems(f"L{layer}_landed", SLOTS)}
        own = (("squared", "basis", "capped", "exped", "logged", "soft"),
               ("act1", "filt2", "act2", "dots", "scaled", "dot"))[layer]
        return by_dma | {k: sem(f"L{layer}_{k}") for k in
                         ("picked", "filt1", "filt", "msg", "window", "added") + own}

    L0, L1 = edge_sems(0), edge_sems(1)
    every = [{k: sems(f"every{n}_{k}", 2) for k in ("onehot", "window", "added")} for n in range(2)]

    block = ctx.enter_context(nc.Block())

    def at(start, size):
        return slice(start, start + size) if isinstance(start, int) else bass.ds(start, size)

    def by_chunk(tile_T, h):
        return tile_T[:, :, :].rearrange("p a b -> p (a b)")[:, at(h.number(HALF_CHUNKS), HALF_CHUNKS)]

    @block.gpsimd
    def _(pool):
        g = nc.gpsimd
        g.memset(ident[:], 0.0).then_inc(s_pool, 1)
        pool.wait_ge(s_pool, 1)
        g.affine_select(out=ident[:], in_=ident[:], compare_op=ALU.not_equal, fill=1.0, base=0,
                        pattern=[[-1, P]], channel_multiplier=1).then_inc(s_ident, 1)
        made = [0]

        def constant(ins):
            made[0] += 1
            ins.then_inc(s_const, 1)
            pool.wait_ge(s_const, made[0])

        pool.wait_ge(s_ident, 1)
        constant(g.memset(ones[:], 1.0))
        constant(g.memset(ones_bf[:], 1.0))
        constant(g.memset(eps[:], LN_EPS))
        constant(g.memset(half_const[:], 0.5))
        constant(g.memset(basis[:], 0.0))
        for part in (neg_centers[0:SPREAD, :], neg_centers[SPREAD:P, :]):
            constant(g.iota(part, [[0, 1]], base=0, channel_multiplier=1,
                            allow_small_or_imprecise_dtypes=True))
        for row, n in ((iota, WINDOW), (windows_iota, all_windows * WINDOW)):
            constant(g.iota(row[:], [[1, n]], base=0, channel_multiplier=0,
                            allow_small_or_imprecise_dtypes=True))
        pool.dma_start(bases[:], dst.rearrange("(a n e) -> a n e", a=1, e=HALF)[:, :, 0],
                     allow_slow_non_contiguous=True)\
            .then_inc(d_bases, 16)
        for s in range(2):
            pool.dma_start(Wf1_sb[s * SPREAD:s * SPREAD + RADIAL, :], Wf1).then_inc(d_weights, 16)
        for w_sb, w in ((Wf2_sb, Wf2), (Wm1_sb, Wm1), (Wm2_sb, Wm2)):
            pool.dma_start(w_sb[:], w).then_inc(d_weights, 16)
        pool.dma_start(bf1_c, bf1.rearrange("(p a) -> p a", a=1)).then_inc(d_bias, 16)
        pool.dma_start(bm1_c, bm1.rearrange("(p a) -> p a", a=1)).then_inc(d_bias, 16)
        for s in range(2):
            pool.dma_start(b0_c[s * HIDDEN:(s + 1) * HIDDEN, :],
                         mlp_b0.rearrange("(p a) -> p a", a=1)).then_inc(d_bias, 16)
            pool.dma_start(b1_c[s * HIDDEN:(s + 1) * HIDDEN, :],
                         mlp_b1.rearrange("(p a) -> p a", a=1)).then_inc(d_bias, 16)
        for i, b in enumerate((bf2, bm2, mlp_b2)):
            pool.dma_start(brow[:, i, :], b.rearrange("(a c) -> a c", a=1)).then_inc(d_bias, 16)

        def table_stored(sm):
            for s in range(2):
                pool.wait_ge(sm["stored"][s], 16 * (last_unit // 2 + (s <= last_unit % 2)))

        def gather(sm, table):
            def step(h):
                if h.parity == 0:
                    wait(pool, sm["picked"], h.pair_upto())
                wait(pool, sm["msg"], h.upto(SLOTS))
                pool.sem_inc(s_gathering, 1)
                for j in range(HALF_CHUNKS):
                    pick = picks[:, h.pair_slot, (h.parity) * HALF_CHUNKS + j:
                                 (h.parity) * HALF_CHUNKS + j + 1]
                    pool.indirect_dma_start(sent[:, h.slot, j, :], None, table,
                                            bass.IndirectOffsetOnAxis(pick, 0))\
                        .then_inc(sm["landed"][h.slot], 16)
            for_halves(pool, iterations, step, 0)

        table_stored(table0)
        gather(L0, h_dram)
        pool.wait_ge(dense0["first"], last_unit + 1)
        pool.wait_ge(s_norm, 3)
        g.memset(sums[:, :, :], 0.0).then_inc(s_zeroed, 1)
        table_stored(table1)
        gather(L1, v_dram)

    @block.sync
    def _(sp):
        sp.dma_start(src_i[:], src.rearrange("(g e) -> g e", e=PAIR)).then_inc(d_rows[0], 16)
        sp.dma_start(W_lin_sb[:], W_lin).then_inc(d_wlin, 16)

        def load_x(u):
            wait(sp, table0["turned"], u.upto(2))
            rows = x[at(u.tile(P), u.cols), :]
            sp.dma_start(unit_in[0:u.rows, u.slot, 0:u.tiles, :],
                         rows.rearrange("(t p) c -> p t c", p=u.rows))\
                .then_inc(table0["loaded"][u.slot], 16)
        each_unit(sp, nodes, load_x)

        sp.wait_ge(s_near, 1)
        sp.dma_start(near_dram.rearrange("(g a) e -> g (a e)", a=2), wt_rows[:]).then_inc(d_near, 16)
        sp.wait_ge(s_weights, 1)
        for part in range(3):
            sp.dma_start(bias3[part:part + 1, :, :], bparts[:, part, :])\
                .then_inc(d_bparts, 16)

        wt_halves = edge_weight.rearrange("(n e) -> n e", e=HALF)

        whole = nodes // P
        pieces = 4
        assert whole % pieces == 0

        def load_features(piece):
            n = whole // pieces
            some = slice(piece * n, (piece + 1) * n)
            rows = x[some.start * P:some.stop * P, :].rearrange("(t p) c -> p t c", p=P)
            sp.dma_start(x_sb[:, some, :], rows).then_inc(d_x, 16)
            if piece == 0 and nodes % P:
                sp.dma_start(x_sb[0:nodes % P, whole, :], x[whole * P:nodes, :]).then_inc(d_x, 16)

        def load_layer1_weights():
            sp.wait_ge(s_blocks, 1)
            for s in range(2):
                sp.dma_start(w0_sb[s * BESSEL:(s + 1) * BESSEL, s * HIDDEN:(s + 1) * HIDDEN], mlp_w0)\
                    .then_inc(d_up, 16)
                sp.dma_start(w1_sb[s * HIDDEN:(s + 1) * HIDDEN, s * HIDDEN:(s + 1) * HIDDEN], mlp_w1)\
                    .then_inc(d_up, 16)
                sp.dma_start(w2_sb[s * HIDDEN:(s + 1) * HIDDEN, :], mlp_w2).then_inc(d_up, 16)
            sp.dma_start(W_up_sb[0:MUL, 0:MUL], W_up0).then_inc(d_up, 16)
            for c in range(3):
                cs = slice(MUL * (c + 1), MUL * (c + 2))
                sp.dma_start(W_up_sb[MUL + c:P:3, cs], W_up1).then_inc(d_up, 16)
                sp.dma_start(W_out_in[cs, 0, :], W_out1[MUL:2 * MUL, :]).then_inc(d_up, 16)
                sp.dma_start(W_out_in[cs, 1, :], W_out1[0:MUL, :]).then_inc(d_up, 16)
            sp.dma_start(W_out_in[0:MUL, 0, :], W_out0[0:MUL, :]).then_inc(d_up, 16)
            sp.dma_start(W_out_in[0:MUL, 1, :], W_out0[MUL:2 * MUL, :]).then_inc(d_up, 16)

        def move_basis(h):
            if h.parity:
                return
            g = h.pair_slot
            b = h.before(2)
            pair_b = b.pair()
            read, stored = h.upto(3), h.uses(32, 1)
            if h.real():
                wait(sp, d_emb[g], stored)
                wait(sp, L0["filt1"], read)
                for s in range(2):
                    first = s * SPREAD
                    sp.dma_start(basis[first:first + RADIAL, g, :],
                                 wt_halves[at(h.number(1, s), 1), :].broadcast_to([RADIAL, HALF]))\
                        .then_inc(L0["r_in"][g], 16)
                    sp.dma_start(basis[first + RADIAL:first + ROWS, g, :],
                                 near_dram[at(h.number(1, s), 1), :].broadcast_to([BESSEL, HALF]))\
                        .then_inc(L0["r_in"][g], 16)
            if b.real():
                g = b.pair_slot
                wait(sp, L0["basis"], b.pair_upto())
                for s in range(2):
                    sp.dma_start(emb_dram[at(pair_b, 1), s * BESSEL:(s + 1) * BESSEL, :]
                                 .rearrange("a k e -> (a k) e"),
                                 basis[s * SPREAD + RADIAL:s * SPREAD + ROWS, g, :])\
                        .then_inc(d_emb[g], 16)
            if h.counter.eng is None and h.pair() < pieces:
                load_features(h.pair())
                if h.pair() == pieces - 1:
                    load_layer1_weights()
        sp.wait_ge(s_const, 9)
        sp.wait_ge(d_near, 16)
        for_halves(sp, iterations, move_basis, 2)

        def load_embedding(h):
            if h.parity:
                return
            g = h.pair_slot
            wait(sp, L1["filt1"], h.pair_upto(2))
            sp.dma_start(emb_in[:, g, :], emb_dram[at(h.pair(), 1), :, :].rearrange("a k e -> (a k) e"))\
                .then_inc(L1["r_in"][g], 16)
        for s in range(2):
            sp.wait_ge(d_emb[s], 32 * iterations)
        for_halves(sp, iterations, load_embedding, 0)

        def store_out(u):
            wait(sp, s_ynorm, u.upto())
            rows = out[at(u.tile(P), u.cols), :]
            sp.dma_start(rows.rearrange("(t p) c -> p t c", p=u.rows),
                         unit_out[0:u.rows, u.slot, 0:u.tiles, :]).then_inc(s_out[u.slot], 16)
        each_unit(sp, nodes, store_out)
        for s in range(2):
            sp.wait_ge(s_out[s], 16 * (last_unit // 2 + (s <= last_unit % 2)))

    @block.scalar
    def _(act):
        a = nc.scalar
        act.dma_start(dst_i[:], dst.rearrange("(g e) -> g e", e=PAIR)).then_inc(d_rows[1], 16)
        act.dma_start(attr, edge_attr.rearrange("(g e) c -> g (e c)", e=PAIR)).then_inc(d_rows[3], 16)
        act.dma_start(wt_rows[:], edge_weight.rearrange("(g e) -> g e", e=PAIR))\
            .then_inc(d_rows[2], 16)
        act.wait_ge(s_wT, 1)
        a.activation(W_linT[:], bank[6][:, 0:P], ACT.Copy).then_inc(s_wTc, 1)

        def copy_tables(sm, table, scale):
            def step(back):
                u, b = back(0), back(2)
                if u is not None:
                    wait(act, sm["turned"], u.upto())
                    wait(act, sm["product"], u.upto(2))
                    a.activation(unit_T[:, u.slot, 0:u.cols], bank[u.slot][:, 0:u.cols], ACT.Copy)\
                        .then_inc(sm["copied"], 1)
                if b is not None:
                    wait(act, sm["product"], b.upto())
                    wait(act, sm["stored"][b.slot], b.uses(16, 1))
                    rows_b = unit_out[0:b.rows, b.slot, 0:b.tiles, :]
                    a.activation(rows_b, quads[2 + b.slot][0:b.rows, 0:b.tiles, :], ACT.Copy,
                                 scale=scale).then_inc(sm["ready"], 1)
                    wait(act, sm["ready"], b.upto())
                    rows = table[at(b.tile(P), b.cols), :].rearrange("(t p) c -> p t c", p=b.rows)
                    act.dma_start(rows, rows_b).then_inc(sm["stored"][b.slot], 16)
            for_units(act, nodes, step, 2)

        copy_tables(table0, h_dram, 1.0)
        act.wait_ge(s_norm, 1)
        a.activation(norm, norm, ACT.Sqrt).then_inc(s_norm, 1)
        a.preload_act_table_set("natural_log_exp_and_others")

        def pick(sm, h):
            for s in range(2):
                wait(act, sm["landed"][h.slot + s], h.uses(64, 1))
            cols2 = srcT[:, :, :].rearrange("p a b -> p (a b)")[:, at(h.number(HALF_CHUNKS), 2 * HALF_CHUNKS)]
            a.activation(picks[:, h.pair_slot, :], cols2, ACT.Copy)\
                .then_inc(sm["picked"], 1)

        def make_basis(h):
            g = h.pair_slot
            used = slice(0, SPREAD + ROWS)
            rows = basis[used, g, :]
            wait(act, L0["r_in"][g], h.uses(64))
            a.activation(rows, rows, ACT.Square, bias=neg_centers[used, :])\
                .then_inc(L0["squared"], 1)
            wait(act, L0["squared"], h.pair_upto())
            a.activation(rows, rows, ACT.Exp, scale=exp_scale[used, :], bias=exp_bias[used, :])\
                .then_inc(L0["basis"], 1)

        def soft_log(sm, parity, n, cols_n, use):
            wait(act, sm["capped"], use)
            tile_ = soft[:, parity, 0:cols_n]
            a.activation(tile_, tile_, ACT.Exp).then_inc(sm[n[0]], 1)
            wait(act, sm[n[0]], use)
            a.activation(tile_, tile_, ACT.Ln, scale=0.5, bias=half_const[:, :])\
                .then_inc(sm[n[1]], 1)

        def layer0(h):
            if h.parity == 0 and h.real():
                pick(L0, h)
                make_basis(h)
            b = h.before(2)
            if b.real():
                soft_log(L0, b.parity, ("exped", "logged"), HALF, b.upto())
        act.wait_ge(s_turned, 2)
        act.wait_ge(s_weights, 1)
        for_halves(act, iterations, layer0, 2)

        def dense_log(u):
            soft_log(dense0, u.slot, ("soft_e", "soft_l"), u.cols, u.upto())
        each_unit(act, nodes, dense_log)

        def root(i):
            act.wait_ge(s_var[i], last_unit + 2)
            a.activation(rstd[:], moments[:, 1, :], ACT.Sqrt, bias=eps[:, :]).then_inc(s_rstd[i], 1)
        root(0)
        copy_tables(table1, v_dram, 1.0 / math.sqrt(MUL))

        def layer1(h):
            if h.parity == 0 and h.real():
                pick(L1, h)
                g = h.pair_slot
                wait(act, L1["filt1"], h.pair_upto())
                wait(act, L1["filt2"], h.pair_upto(2))
                a.activation(h1[:, g, :], bank[0][:], ACT.Silu, bias=b0_c).then_inc(L1["act1"], 1)
            if h.parity == 1:
                b = h.before(1)
                if b.real():
                    g = b.pair_slot
                    wait(act, L1["filt2"], b.pair_upto())
                    wait(act, L1["filt"], b.upto(3))
                    a.activation(h2[:, g, :], bank[1][:], ACT.Silu, bias=b1_c)\
                        .then_inc(L1["act2"], 1)
        for_halves(act, iterations, layer1, 0)

        def stage_sums(u):
            wait(act, dense1["second"], u.upto(2))
            n = u.cols
            a.activation(stage[:, u.slot, :, 0:n], sums[:, :, at(u.tile(P), n)], ACT.Copy)\
                .then_inc(dense1["staged"], 1)
        act.wait_ge(L1["added"], halves)
        each_unit(act, nodes, stage_sums)
        root(1)

    @block.tensor
    def _(pe):
        t_ = nc.tensor
        pe.wait_ge(s_ident, 1)
        pe.wait_ge(d_wlin, 16)
        t_.transpose(bank[6][:, 0:P], W_lin_sb[:], ident[:]).then_inc(s_wT, 1)

        turns = [0]

        def turn_rows(rows):
            if turns[0] >= 2:
                pe.wait_ge(s_turned, turns[0] - 1)
            for j, r in enumerate(rows):
                last = t_.transpose(quads[6 + turns[0] % 2][:, j, 0:pairs], r,
                                    ident[0:pairs, 0:pairs])
            last.then_inc(s_turn, 1)
            turns[0] += 1

        def turn_all(tile_rows):
            for j in range(0, pair_chunks, 4):
                turn_rows([tile_rows[:, (j + i) * P:(j + i + 1) * P] for i in range(4)])

        pe.wait_ge(s_wTc, 1)
        pe.wait_ge(s_dve, 1)
        turn_all(src_f)
        pe.wait_ge(s_dve, 2)
        turn_all(dst_f[:, :])
        pe.wait_ge(d_rows[3], 16)
        for c in range(3):
            turn_rows([attr[:, j * P * 3 + c:((j + 1) * P - 1) * 3 + c + 1:3] for j in range(4)])
            turn_rows([attr[:, j * P * 3 + c:((j + 1) * P - 1) * 3 + c + 1:3] for j in range(4, 8)])
        pe.wait_ge(s_dve, 3)
        turn_all(rel2)

        def turn_unit(sm, u):
            if sm is table0:
                wait(pe, sm["loaded"][u.slot], u.uses(16))
            else:
                wait(pe, sm["normed"], u.upto())
            wait(pe, sm["copied"], u.upto(2))
            for t in range(u.tiles):
                last = t_.transpose(bank[u.slot][:, t * P:t * P + u.rows],
                                    unit_in[0:u.rows, u.slot, t, :], ident[0:u.rows, 0:u.rows])
            last.then_inc(sm["turned"], 1)

        def product_unit(sm, u, weight):
            wait(pe, sm["copied"], u.upto())
            wait(pe, sm["ready"], u.upto(2))
            for t in range(u.tiles):
                last = t_.matmul(quads[2 + u.slot][0:u.rows, t, :],
                                 unit_T[:, u.slot, t * P:t * P + u.rows], weight[:],
                                 start=True, stop=True)
            last.then_inc(sm["product"], 1)

        def tables(sm, weight):
            def step(back):
                if back(0) is not None:
                    turn_unit(sm, back(0))
                if back(1) is not None:
                    product_unit(sm, back(1), weight)
            for_units(pe, nodes, step, 1)

        tables(table0, W_linT)

        pe.wait_ge(s_fits, 1)
        pe.wait_ge(s_const, 1)
        pe.wait_ge(s_turned, 12)
        t_.matmul(bank[6][0:1, 0:1], fits_row[:], ones[0:pairs, :], start=True, stop=True)\
            .then_inc(s_flag, 1)

        def products(out_bank, n_tiles, rows, lhs, weight, which):
            for j in range(n_tiles):
                t_.matmul(out_bank[0:rows, j, :], lhs(j), weight, start=(j == 0), stop=False,
                          skip_group_check=True)
            return t_.matmul(out_bank[0:rows, 0:n_tiles, :], ones_bf[:, 0:rows],
                             bias3[:, which:which + 1, :].broadcast_to([3, n_tiles, P]),
                             start=False, stop=True, skip_group_check=True)

        def window_sums(sm, h, outputs):
            p = h.parity
            wait(pe, sm["msg"], h.upto())
            b = h.before(2)
            wait(pe, sm["added"], b.upto())
            ps = winps[p][:, :].rearrange("p (k n) -> p k n", n=WINDOW)
            for k in range(outputs):
                for j in range(HALF_CHUNKS):
                    last = t_.matmul(ps[:, k, :], msg[:, p, j, k * P:(k + 1) * P],
                                     onehot[:, p, j, :], start=(j == 0),
                                     stop=(j == HALF_CHUNKS - 1))
            last.then_inc(sm["window"], 1)

        def every_window(sm, ev, h, outputs):
            p = h.parity
            first = h.number(all_windows // 2)
            with pe.Fori(1, all_windows // 2 + 1) as i:
                use = pe.snap(i + first)
                wait(pe, sm["msg"], h.upto())
                for q in range(2):
                    ps = winps[q][:, :].rearrange("p (k n) -> p k n", n=WINDOW)
                    pe.wait_ge(ev["onehot"][q], use)
                    pe.wait_ge(ev["added"][q], use)
                    for k in range(outputs):
                        for j in range(HALF_CHUNKS):
                            last = t_.matmul(ps[:, k, :], msg[:, p, j, k * P:(k + 1) * P],
                                             onehot[:, q, j, :], start=(j == 0),
                                             stop=(j == HALF_CHUNKS - 1))
                    last.then_inc(ev["window"][q], 1)

        def hidden0(h):
            p, g = h.parity, h.pair_slot
            b = h.before(SLOTS)
            wait(pe, L0["basis"], h.pair_upto())
            wait(pe, L0["soft"], b.upto())
            rows = slice(p * SPREAD, p * SPREAD + RADIAL)
            t_.matmul(filtA[h.slot][:, :], Wf1_sb[rows, :], basis[rows, g, :], start=True, stop=True)\
                .then_inc(L0["filt1"], 1)

        def filter0(h):
            p = h.parity
            b = h.before(2)
            wait(pe, L0["msg"], b.upto())
            wait(pe, L0["soft"], h.upto())
            products(filtB[p], HALF_CHUNKS, P, lambda j: hid[:, p, j * P:(j + 1) * P], Wf2_sb[:], 0)\
                .then_inc(L0["filt"], 1)

        def hidden1(h):
            g = h.pair_slot
            wait(pe, L1["r_in"][g], h.uses(16))
            b = h.before(2)
            wait(pe, L1["act1"], b.pair_upto())
            t_.matmul(bank[0][:, :], w0_sb[:], emb_in[:, g, :], start=True, stop=True)\
                .then_inc(L1["filt1"], 1)

        def second1(h):
            g = h.pair_slot
            wait(pe, L1["act1"], h.pair_upto())
            b = h.before(2)
            wait(pe, L1["act2"], b.pair_upto())
            t_.matmul(bank[1][:, :], w1_sb[:], h1[:, g, :], start=True, stop=True)\
                .then_inc(L1["filt2"], 1)

        def filter1(h):
            p, g = h.parity, h.pair_slot
            b = h.before(2)
            wait(pe, L1["msg"], b.upto())
            wait(pe, L1["act2"], h.pair_upto())
            rows = slice(p * HIDDEN, (p + 1) * HIDDEN)
            products(filtB[p], HALF_CHUNKS, P, lambda j: h2[rows, g, j * P:(j + 1) * P],
                     w2_sb[rows, :], 2).then_inc(L1["filt"], 1)

        def layer0(h):
            if h.real():
                hidden0(h)
            b = h.before(3)
            if b.real():
                filter0(b)
            b = h.before(5)
            if b.real():
                window_sums(L0, b, 1)

        def layer1(h):
            if h.parity == 0 and h.real():
                hidden1(h)
            b = h.before(1)
            if h.parity == 1 and b.real():
                second1(b)
            b = h.before(3)
            if b.real():
                filter1(b)
            b = h.before(5)
            if b.real():
                window_sums(L1, b, 2)

        def layer0_any(h):
            hidden0(h)
            filter0(h)
            every_window(L0, every[0], h, 1)

        def layer1_any(h):
            if h.parity == 0:
                hidden1(h)
                second1(h)
            filter1(h)
            every_window(L1, every[1], h, 2)

        def tables_read(sm):
            pe.wait_ge(sm["ready"], last_unit + 1)
        tables_read(table0)
        pe.wait_ge(d_weights, 16 * 5)
        pe.wait_ge(d_bparts, 48)
        pe.wait_ge(s_flag, 2)
        flag = pe.value_load(sorted_flag[0:1, 0:1], min_val=0, max_val=1)
        with pe.If(flag):
            for_halves(pe, iterations, layer0, 5)
        with pe.Else():
            for_halves(pe, iterations, layer0_any, 0)

        def dense_first(u):
            n = u.cols
            wait(pe, dense0["hidden"], u.upto(2))
            t_.matmul(filtA[u.slot][:, 0:n], Wm1_sb[:], sums[:, 0, at(u.tile(P), n)],
                      start=True, stop=True).then_inc(dense0["first"], 1)

        def dense_second(u):
            wait(pe, dense0["added"], u.upto(2))
            wait(pe, dense0["hidden"], u.upto())
            products(filtB[u.slot], u.tiles, u.rows,
                     lambda t: hid[:, u.slot, t * P:t * P + u.rows], Wm2_sb[:], 1)\
                .then_inc(dense0["second"], 1)

        def dense(back):
            if back(0) is not None:
                dense_first(back(0))
            if back(2) is not None:
                dense_second(back(2))
        pe.wait_ge(L0["added"], halves)
        for_units(pe, nodes, dense, 2)
        pe.wait_ge(d_up, 16 * 18)
        tables(table1, W_up_sb)
        tables_read(table1)
        flag = pe.value_load(sorted_flag[0:1, 0:1], min_val=0, max_val=1)
        with pe.If(flag):
            for_halves(pe, iterations, layer1, 5)
        with pe.Else():
            for_halves(pe, iterations, layer1_any, 0)

        def outputs(u):
            wait(pe, dense1["staged"], u.upto())
            wait(pe, dense1["added"], u.upto(2))
            for t in range(u.tiles):
                for k, w in enumerate((W_outA, W_outB)):
                    last = t_.matmul(filtB[u.slot][0:u.rows, t, :],
                                     stage[:, u.slot, k, t * P:t * P + u.rows], w[:],
                                     start=(k == 0), stop=(k == 1))
            last.then_inc(dense1["second"], 1)
        pe.wait_ge(s_weights, 2)
        each_unit(pe, nodes, outputs)

    @block.vector
    def _(dve):
        v = nc.vector
        steps = [0]

        def then(ins):
            steps[0] += 1
            ins.then_inc(s_own, 1)
            dve.wait_ge(s_own, steps[0])

        turned = [0]

        def copy_turn(tile_T):
            for j in (0, 4):
                turned[0] += 1
                dve.wait_ge(s_turn, turned[0])
                v.tensor_copy(tile_T[:, :, j:j + 4].rearrange("p g j -> p j g"),
                              quads[6 + (turned[0] - 1) % 2][:, :, 0:pairs]).then_inc(s_turned, 1)

        for w_sb in (w0_sb, w1_sb, W_up_sb, W_outA, W_outB):
            last = v.memset(w_sb[:], 0.0)
        last.then_inc(s_blocks, 1)
        dve.wait_ge(d_rows[0], 16)
        v.tensor_copy(src_f, src_i[:]).then_inc(s_dve, 1)
        dve.wait_ge(d_rows[1], 16)
        v.tensor_copy(dst_f[:], dst_i[:]).then_inc(s_dve, 1)
        copy_turn(srcT)
        dve.wait_ge(s_dve, 2)
        d3 = dst_f[:, :].rearrange("g (a b) -> g a b", b=HALF)
        v.tensor_tensor(rel_f, d3, d3[:, :, 0:1].broadcast_to([pairs, 2, HALF]),
                        ALU.subtract).then_inc(s_dve, 1)
        copy_turn(dstT)
        for c in range(3):
            copy_turn(dirT[:, :, :, c])
        copy_turn(relT)
        dve.wait_ge(d_rows[2], 16)
        then(v.tensor_scalar(beyond, wt_rows[:], 1.0, FAR, ALU.is_gt, ALU.mult))
        v.scalar_tensor_tensor(out=wt_rows[:], in0=wt_rows[:], scalar=0.0, in1=beyond, op0=ALU.max,
                               op1=ALU.add).then_inc(s_near, 1)
        dve.wait_ge(s_turned, 12)
        raw = dirT[:, :, :, :].rearrange("p g j c -> p (g j c)")
        then(v.tensor_tensor(squares, raw, raw, ALU.mult))
        v.tensor_reduce(norm, squares.rearrange("p (e c) -> p e c", c=3), AXES.X, ALU.add)\
            .then_inc(s_norm, 1)
        then(v.tensor_scalar(fits, rel2, 0.0, None, ALU.is_ge))
        then(v.scalar_tensor_tensor(out=fits, in0=rel2, scalar=float(WINDOW), in1=fits,
                                    op0=ALU.is_lt, op1=ALU.mult))
        then(v.scalar_tensor_tensor(out=fits, in0=dst_f[:], scalar=float(nodes), in1=fits,
                                    op0=ALU.is_ge, op1=ALU.max))
        v.tensor_reduce(fits_row[:], fits, AXES.X, ALU.min).then_inc(s_fits, 1)

        then(v.memset(sums[:, 0, :], 0.0))
        dve.wait_ge(s_const, 9)
        delta = np.float32(CUTOFF) / np.float32(RADIAL - 1)
        number = neg_centers
        then(v.tensor_scalar(is_radial[:], number[:], float(RADIAL), None, ALU.is_lt))
        then(v.tensor_scalar(is_bessel[:], number[:], float(RADIAL), None, ALU.is_ge))
        then(v.tensor_scalar(exp_bias[:], number[:], -float(RADIAL), -1.0 / (BESSEL - 1), ALU.add,
                             ALU.mult))
        then(v.tensor_tensor(exp_bias[:], exp_bias[:], is_bessel[:], ALU.mult))
        then(v.scalar_tensor_tensor(out=number[:], in0=number[:], scalar=-float(delta),
                                    in1=is_radial[:], op0=ALU.mult, op1=ALU.mult))
        then(v.tensor_tensor(neg_centers[:], number[:], exp_bias[:], ALU.add))
        then(v.tensor_scalar(exp_bias[:], is_bessel[:], 0.5 * math.log(BESSEL), None, ALU.mult))
        then(v.tensor_scalar(exp_scale[:], is_radial[:], -float(1.0 / (2.0 * delta * delta)), None,
                             ALU.mult))
        then(v.scalar_tensor_tensor(out=exp_scale[:], in0=is_bessel[:],
                                    scalar=-0.5 * (BESSEL - 1) ** 2, in1=exp_scale[:],
                                    op0=ALU.mult, op1=ALU.add))
        dve.wait_ge(d_bias, 16 * 9)
        then(v.tensor_scalar(bf1_s, bf1_c, -math.log(2.0), None, ALU.add))
        then(v.tensor_scalar(bm1_s, bm1_c, -math.log(2.0), None, ALU.add))
        b_all = brow[:, :, :].rearrange("a b c -> a (b c)")
        r_all = brest[:, :, :].rearrange("a b c -> a (b c)")
        then(v.tensor_copy(bparts[:, 0, :], b_all))
        then(v.tensor_tensor(r_all, b_all, bparts[:, 0, :], ALU.subtract))
        then(v.tensor_copy(bparts[:, 1, :], r_all))
        then(v.tensor_tensor(r_all, r_all, bparts[:, 1, :], ALU.subtract))
        v.tensor_copy(bparts[:, 2, :], r_all).then_inc(s_weights, 1)
        dve.wait_ge(s_flag, 1)
        v.tensor_scalar(sorted_flag[:], bank[6][0:1, 0:1], pairs - 0.5, None, ALU.is_ge)\
            .then_inc(s_flag, 1)
        dve.wait_ge(s_norm, 2)
        then(v.tensor_scalar(norm, norm, 1e-12, None, ALU.add))
        then(v.reciprocal(norm, norm))
        v.tensor_tensor(raw.rearrange("p (e c) -> p e c", c=3), raw.rearrange("p (e c) -> p e c", c=3),
                        norm.rearrange("p (e a) -> p e a", a=1).broadcast_to([P, all_chunks, 3]),
                        ALU.mult).then_inc(s_norm, 1)

        def one_hots(h, sm):
            p = h.parity
            b = h.before(2)
            wait(dve, sm["window"], b.upto())
            v.tensor_tensor(onehot[:, p],
                            by_chunk(relT, h).rearrange("p (j a) -> p j a", a=1)
                            .broadcast_to([P, HALF_CHUNKS, WINDOW]),
                            iota[:, :].rearrange("p (a n) -> p a n", a=1)
                            .broadcast_to([P, HALF_CHUNKS, WINDOW]), ALU.is_equal)

        def add_window(sm, h, outputs, base):
            ps = winps[h.parity][:, :].rearrange("p (k n) -> p k n", n=WINDOW)
            wait(dve, sm["window"], h.upto())
            b = h.before(1)
            wait(dve, sm["added"], b.upto())
            here = sums[:, 0:outputs, at(base, WINDOW)]
            v.tensor_tensor(here, here, ps[:, 0:outputs, :], ALU.add).then_inc(sm["added"], 1)

        def cap0(h):
            p = h.parity
            b = h.before(2)
            wait(dve, L0["soft"], b.upto())
            wait(dve, L0["filt1"], h.upto())
            v.tensor_scalar(soft[:, p, :], filtA[h.slot][:, :], bf1_c, EXP_CAP, ALU.add, ALU.min)\
                .then_inc(L0["capped"], 1)

        def soft0(h):
            p = h.parity
            b = h.before(2)
            wait(dve, L0["filt"], b.upto())
            wait(dve, L0["logged"], h.upto())
            v.scalar_tensor_tensor(out=hid[:, p, :], in0=filtA[h.slot][:, :], scalar=bf1_s,
                                   in1=soft[:, p, :], op0=ALU.add, op1=ALU.max)\
                .then_inc(L0["soft"], 1)

        def msg0(h):
            p = h.parity
            wait(dve, L0["filt"], h.upto())
            wait(dve, L0["landed"][h.slot], h.uses(64))
            b = h.before(2)
            wait(dve, L0["window"], b.upto())
            v.tensor_tensor(msg[:, p, :, 0:P], filtB[p], sent[:, h.slot], ALU.mult)\
                .then_inc(L0["msg"], 1)

        def msg1(h):
            p = h.parity
            filt = filtB[p].rearrange("p j (i m) -> p j i m", m=MUL)
            rows = sent[:, h.slot]
            vec = rows[:, :, MUL:].rearrange("p j (c m) -> p j c m", m=MUL)
            cube = [P, HALF_CHUNKS, 3, MUL]
            dirs = dirT[:, :, :, :].rearrange("p a b c -> p (a b) c")[:, at(h.number(HALF_CHUNKS), HALF_CHUNKS), :]\
                .rearrange("p j (c m) -> p j c m", m=1).broadcast_to(cube)
            wait(dve, L1["landed"][h.slot], h.uses(64))
            v.tensor_tensor(dots[:, p], vec, dirs, ALU.mult).then_inc(L1["dots"], 1)
            wait(dve, L1["filt"], h.upto())
            b = h.before(2)
            wait(dve, L1["window"], b.upto())
            scaled = msg[:, p, :, :].rearrange("p j (q m) -> p j q m", m=MUL)[:, :, 0:9:8, :]
            v.tensor_tensor(scaled, filt[:, :, 0:2, :],
                            rows[:, :, 0:MUL].rearrange("p j (a m) -> p j a m", a=1)
                            .broadcast_to([P, HALF_CHUNKS, 2, MUL]), ALU.mult)\
                .then_inc(L1["scaled"], 1)
            wait(dve, L1["dots"], h.upto())
            v.tensor_reduce(dot[:, p], dots[:, p].rearrange("p j c m -> p j m c"), AXES.X, ALU.add)\
                .then_inc(L1["dot"], 1)
            v.tensor_tensor(msg[:, p, :, MUL:P].rearrange("p j (c m) -> p j c m", m=MUL), vec,
                            filt[:, :, 2:3, :].broadcast_to(cube), ALU.mult)
            wait(dve, L1["scaled"], h.upto())
            v.tensor_tensor(msg[:, p, :, P + MUL:2 * P].rearrange("p j (c m) -> p j c m", m=MUL),
                            msg[:, p, :, 2 * P:].rearrange("p j (a m) -> p j a m", a=1)
                            .broadcast_to(cube), dirs, ALU.mult)
            wait(dve, L1["dot"], h.upto())
            v.tensor_tensor(msg[:, p, :, P:P + MUL], filt[:, :, 3, :], dot[:, p], ALU.mult)\
                .then_inc(L1["msg"], 1)

        def loop_layer(step, lag):
            def load_bases(first, n):
                if n <= 0:
                    return []
                _, values = nc.values_load_multi_w_load_instructions(
                    bases[0:1, at(first, n)], engines=[mybir.EngineType.DVE], min_val=0,
                    max_val=width - WINDOW, skip_runtime_bounds_check_because="receivers are nodes")
                return values
            count = iterations * SLOTS
            peeled = min(2, iterations)

            def steps_of(halves_, first, values):
                for i, h in enumerate(halves_):
                    step(h, values[i + first] if i + first >= 0 else None)

            for it in range(peeled):
                first = it * SLOTS - lag
                values = load_bases(max(first, 0), first + SLOTS - max(first, 0))
                steps_of([Half(it * SLOTS + s, count) for s in range(SLOTS)], min(first, 0), values)
            if iterations > peeled:
                with dve.Fori(peeled, iterations) as it:
                    counter = Counter(dve, it)
                    values = load_bases(counter.value(SLOTS, -lag), SLOTS)
                    steps_of([Half(s, count, counter) for s in range(SLOTS)], 0, values)
            values = load_bases(count - lag, lag)
            steps_of([Half(n, count) for n in range(count, count + lag)], 0, values)

        def layer0(h, base):
            b1, b2, b4, b6 = (h.before(i) for i in (1, 2, 4, 6))
            if b1.real():
                cap0(b1)
            if b4.real():
                one_hots(b4, L0)
                msg0(b4)
            if b6.real():
                add_window(L0, b6, 1, base)
            if b2.real():
                soft0(b2)

        def layer1(h, base):
            b4, b6 = h.before(4), h.before(6)
            if b6.real():
                add_window(L1, b6, 2, base)
            if b4.real():
                one_hots(b4, L1)
                msg1(b4)

        def every_window(sm, ev, h, outputs):
            first = h.number(all_windows // 2)
            targets = by_chunk(dstT, h)

            def hots(i, q):
                lo = i * (2 * WINDOW) + (q - 2) * WINDOW
                v.tensor_tensor(onehot[:, q],
                                targets.rearrange("p (j a) -> p j a", a=1)
                                .broadcast_to([P, HALF_CHUNKS, WINDOW]),
                                windows_iota[:, bass.ds(lo, WINDOW)]
                                .rearrange("p (a n) -> p a n", a=1)
                                .broadcast_to([P, HALF_CHUNKS, WINDOW]), ALU.is_equal)\
                    .then_inc(ev["onehot"][q], 1)

            with dve.Fori(1, all_windows // 2 + 1) as i:
                use = dve.snap(i + first)
                more = dve.snap(use + 1)
                for q in range(2):
                    dve.wait_ge(ev["window"][q], use)
                    hots(i, q)
                for q in range(2):
                    ps = winps[q][:, :].rearrange("p (k n) -> p k n", n=WINDOW)
                    here = sums[:, 0:outputs, bass.ds(i * (2 * WINDOW) + (q - 2) * WINDOW, WINDOW)]
                    dve.wait_ge(ev["window"][q], more)
                    v.tensor_tensor(here, here, ps[:, 0:outputs, :], ALU.add)\
                        .then_inc(ev["added"][q], 1)
            dve.sem_inc(sm["window"], 1)
            dve.wait_ge(ev["added"][1], h.number(all_windows // 2, all_windows // 2 + 1))
            dve.sem_inc(sm["added"], 1)

        def layer0_any(h):
            cap0(h)
            soft0(h)
            msg0(h)
            every_window(L0, every[0], h, 1)

        def layer1_any(h):
            msg1(h)
            every_window(L1, every[1], h, 2)

        dve.wait_ge(d_bases, 16)
        dve.wait_ge(s_flag, 2)
        flag = dve.value_load(sorted_flag[0:1, 0:1], min_val=0, max_val=1)
        with dve.If(flag):
            loop_layer(layer0, 6)
        with dve.Else():
            for q in range(2):
                dve.sem_inc(every[0]["window"][q], 1)
                dve.sem_inc(every[0]["added"][q], 1)
            for_halves(dve, iterations, layer0_any, 0)

        def norm_stats(sm, u, moved):
            rows = slice(0, u.rows)
            here = x_sb[rows, at(u.tile(), u.tiles), :]
            v.tensor_tensor(here, filtB[u.slot][rows, 0:u.tiles, :], here, ALU.add)\
                .then_inc(sm["added"], 1)
            wait(dve, sm["added"], u.upto())
            dve.sem_inc(s_measuring, 1)
            for t in range(u.tiles):
                last = v.bn_stats(stats[rows, u.slot, t, :],
                                  x_sb[rows, at(u.tile(1, t), 1), :].rearrange("p a c -> p (a c)"))
            last.then_inc(sm["stats"], 1)
            wait(dve, sm["stats"], u.upto())
            v.tensor_scalar(all_stats[rows, at(u.tile(), u.tiles), :], stats[rows, u.slot, 0:u.tiles],
                            1.0, None, ALU.mult).then_inc(moved, 1)

        def dense(back):
            u = back(0)
            if u is not None:
                n = u.cols
                wait(dve, dense0["hidden"], u.upto(2))
                wait(dve, dense0["first"], u.upto())
                v.tensor_scalar(soft[:, u.slot, 0:n], filtA[u.slot][:, 0:n], bm1_c, EXP_CAP,
                                ALU.add, ALU.min).then_inc(dense0["capped"], 1)
            u = back(1)
            if u is not None:
                n = u.cols
                wait(dve, dense0["soft_l"], u.upto())
                wait(dve, dense0["second"], u.upto(2))
                v.scalar_tensor_tensor(out=hid[:, u.slot, 0:n], in0=filtA[u.slot][:, 0:n],
                                       scalar=bm1_s, in1=soft[:, u.slot, 0:n], op0=ALU.add,
                                       op1=ALU.max).then_inc(dense0["hidden"], 1)
            if back(3) is not None:
                wait(dve, dense0["second"], back(3).upto())
                norm_stats(dense0, back(3), s_var[0])
        dve.wait_ge(d_up, 16 * 18)
        out_scale = 1.0 / (math.sqrt(2 * MUL) * AVG_DEGREE)
        root3 = math.sqrt(3.0)
        for k, w_sb in enumerate((W_outA, W_outB)):
            v.tensor_scalar(w_sb[0:MUL, 0:MUL], W_out_in[0:MUL, k, :], out_scale, None, ALU.mult)
            for c in range(3):
                cs = slice(MUL * (c + 1), MUL * (c + 2))
                last = v.tensor_scalar(w_sb[cs, MUL + c:P:3], W_out_in[cs, k, :],
                                       out_scale * (root3 if k else 1.0), None, ALU.mult)
        last.then_inc(s_weights, 1)
        dve.wait_ge(d_x, 16 * (4 + bool(nodes % P)))
        then(v.memset(all_stats[:], 0.0))
        for_units(dve, nodes, dense, 3)

        def invert(i):
            mean, var, diff = (moments[:, m, :] for m in range(3))
            even, odd = all_stats[:, :, 1], all_stats[:, :, 4]
            dve.wait_ge(s_var[i], last_unit + 1)
            then(v.tensor_tensor(mean, even, odd, ALU.add))
            then(v.tensor_scalar(mean, mean, 0.5, None, ALU.mult))
            then(v.tensor_tensor(diff, even, mean, ALU.subtract))
            then(v.tensor_tensor(diff, diff, diff, ALU.mult))
            then(v.tensor_tensor(var, all_stats[:, :, 2], all_stats[:, :, 5], ALU.add))
            v.scalar_tensor_tensor(out=var, in0=var, scalar=1.0 / P, in1=diff, op0=ALU.mult,
                                   op1=ALU.add).then_inc(s_var[i], 1)
            dve.wait_ge(s_rstd[i], 1)
            v.reciprocal(rstd[:], rstd[:]).then_inc(s_rstd[i], 1)
            dve.wait_ge(s_rstd[i], 2)

        def normalise(u, target, t):
            rows = slice(0, u.rows)
            col = u.tile(1, t)
            return v.tensor_scalar(target, x_sb[rows, at(col, 1), :].rearrange("p a c -> p (a c)"),
                                   moments[rows, 0, at(col, 1)],
                                   rstd[rows, at(col, 1)], ALU.subtract, ALU.mult)

        invert(0)

        def norm_rows(u):
            rows = slice(0, u.rows)
            wait(dve, table1["turned"], u.upto(2))
            for t in range(u.tiles):
                last = normalise(u, unit_in[rows, u.slot, t, :], t)
            last.then_inc(table1["normed"], 1)
            wait(dve, table1["normed"], u.upto())
            v.tensor_scalar(x_sb[rows, at(u.tile(), u.tiles), :],
                            unit_in[rows, u.slot, 0:u.tiles, :], 1.0, None, ALU.mult)
        each_unit(dve, nodes, norm_rows)

        dve.wait_ge(s_zeroed, 1)
        flag = dve.value_load(sorted_flag[0:1, 0:1], min_val=0, max_val=1)
        with dve.If(flag):
            loop_layer(layer1, 6)
        with dve.Else():
            for q in range(2):
                dve.sem_inc(every[1]["window"][q], 1)
                dve.sem_inc(every[1]["added"][q], 1)
            for_halves(dve, iterations, layer1_any, 0)

        def residual1(u):
            wait(dve, dense1["second"], u.upto())
            norm_stats(dense1, u, s_var[1])
        each_unit(dve, nodes, residual1)
        invert(1)

        def finish(u):
            rows = slice(0, u.rows)
            wait(dve, s_out[u.slot], u.uses(16, 1))
            for t in range(u.tiles):
                last = normalise(u, unit_out[rows, u.slot, t, :], t)
            last.then_inc(s_ynorm, 1)
        each_unit(dve, nodes, finish)


def kernel(**inputs):
    import concourse.bacc as bacc
    from concourse.bass_utils import run_bass_kernel_spmd

    x = np.ascontiguousarray(inputs["x"])
    nodes = x.shape[0]
    edges = inputs["src"].shape[0]
    more = padded_edges(edges) - edges
    arrays = {"x": x}
    for name, fill in (("src", 0), ("dst", pad_receiver(nodes)), ("edge_attr_3", 0),
                       ("edge_weight", 0)):
        a = np.asarray(inputs[name])
        tail = np.full((more,) + a.shape[1:], fill, a.dtype)
        arrays[name] = np.ascontiguousarray(np.concatenate([a, tail]))
    for name in ("L0_gnn_W_lin", "L0_gnn_Wf1", "L0_gnn_bf1", "L0_gnn_Wf2", "L0_gnn_bf2",
                 "L0_gnn_Wm1", "L0_gnn_bm1", "L0_gnn_Wm2", "L0_gnn_bm2", "L1_gnn_W_up0",
                 "L1_gnn_W_up1", "L1_gnn_mlp_w0", "L1_gnn_mlp_b0", "L1_gnn_mlp_w1",
                 "L1_gnn_mlp_b1", "L1_gnn_mlp_w2", "L1_gnn_mlp_b2", "L1_gnn_W_out0",
                 "L1_gnn_W_out1"):
        arrays[name] = np.ascontiguousarray(inputs[name])
    nc = bacc.Bacc("TRN2", target_bir_lowering=False, num_devices=1)
    args = [nc.dram_tensor(f"in_{k}", a.shape, mybir.dt.from_np(a.dtype), kind="ExternalInput").ap()
            for k, a in arrays.items()]
    args.append(nc.dram_tensor("out", x.shape, F32, kind="ExternalOutput").ap())
    with ExitStack() as ctx:
        build(nc, *args, ctx)
    r = run_bass_kernel_spmd(nc, [{f"in_{k}": a for k, a in arrays.items()}], core_ids=[0])
    return r.results[0]["out"]
```

```python
from contextlib import ExitStack
import math

import numpy as np
import concourse.bass as bass
from concourse import mybir

F32 = mybir.dt.float32
BF16 = mybir.dt.bfloat16
I32 = mybir.dt.int32
I16 = mybir.dt.int16
ALU = mybir.AluOpType
ACT = mybir.ActivationFunctionType
AXES = mybir.AxisListType

P = 128
HALF_CHUNKS = 4
HALF = HALF_CHUNKS * P
SLOTS = 4
PAIR = 2 * HALF
WINDOW = 128
UNIT_TILES = 4
WIDE = 4
FEATURE_LOADS = 4
LN_EPS = 1e-5
EXP_CAP = 40.0

RADIAL, CUTOFF = 50, 5.0
BESSEL = 8
MUL = 32
HIDDEN = 64
AVG_DEGREE = 16.0
SPREAD = 64
ROWS = RADIAL + BESSEL
FAR = 8.0


def padded_edges(edges):
    return -(-edges // (SLOTS * HALF)) * SLOTS * HALF


def pad_receiver(nodes):
    return -(-nodes // P) * P


class Counter:

    def __init__(self, eng=None, it=0):
        self.eng, self.it, self.known = eng, it, {}

    def value(self, scale, offset):
        if self.eng is None:
            return offset
        if (scale, offset) not in self.known:
            self.known[scale, offset] = self.eng.snap(self.it * scale + offset)
        return self.known[scale, offset]


class Half:

    def __init__(self, rel, count, counter=None):
        self.rel, self.count, self.counter = rel, count, counter or Counter()
        self.slot, self.pair_slot, self.parity = rel % SLOTS, rel // 2 % 2, rel % 2

    def real(self):
        return self.counter.eng is not None or 0 <= self.rel < self.count

    def before(self, k):
        return Half(self.rel - k, self.count, self.counter)

    def number(self, scale=1, plus=0):
        return self.counter.value(SLOTS * scale, self.rel * scale + plus)

    def upto(self, back=0):
        return self.counter.value(SLOTS, self.rel + 1 - back)

    def pair_upto(self, back=0):
        return self.counter.value(SLOTS // 2, self.rel // 2 + 1 - back)

    def pair(self):
        return self.counter.value(SLOTS // 2, self.rel // 2)

    def uses(self, scale, back=0):
        return self.counter.value(scale, (self.rel // SLOTS + 1 - back) * scale)


def wait(eng, sem, value):
    if not isinstance(value, int) or value > 0:
        eng.wait_ge(sem, value)


def for_halves(eng, iterations, step, behind):
    count = iterations * SLOTS
    peeled = min(2, iterations)
    for n in range(peeled * SLOTS):
        step(Half(n, count))
    if iterations > peeled:
        with eng.Fori(peeled, iterations) as it:
            counter = Counter(eng, it)
            for s in range(SLOTS):
                step(Half(s, count, counter))
    for n in range(count, count + behind):
        step(Half(n, count))


class Unit:

    def __init__(self, rel, tiles, rows, counter=None):
        self.rel, self.tiles, self.rows, self.counter = rel, tiles, rows, counter or Counter()
        self.slot, self.wide_slot = rel % 2, rel % WIDE
        self.cols = tiles * P if rows == P else rows

    def upto(self, back=0):
        return self.counter.value(WIDE, self.rel + 1 - back)

    def uses(self, scale):
        return self.counter.value(scale, (self.rel // WIDE + 1) * scale)

    def tile(self, scale=1, plus=0):
        return self.counter.value(WIDE * UNIT_TILES * scale, self.rel * UNIT_TILES * scale + plus)


def fixed_unit(number, nodes):
    if number < 0 or number * UNIT_TILES * P >= nodes:
        return None
    left = nodes - number * UNIT_TILES * P
    tiles = min(UNIT_TILES, -(-left // P))
    assert tiles == 1 or left >= tiles * P
    return Unit(number, tiles, min(P, left))


def for_units(eng, nodes, step, behind):
    whole = nodes // (UNIT_TILES * P) // WIDE
    units = -(-nodes // (UNIT_TILES * P))
    peeled = min(1, whole)
    for n in range(WIDE * peeled):
        step(lambda k: fixed_unit(n - k, nodes))
    if whole > peeled:
        with eng.Fori(peeled, whole) as it:
            counter = Counter(eng, it)
            for s in range(WIDE):
                step(lambda k: Unit(s - k, UNIT_TILES, P, counter))
    for n in range(WIDE * whole, units + behind):
        step(lambda k: fixed_unit(n - k, nodes))


def each_unit(eng, nodes, step):
    def own(back):
        if back(0) is not None:
            step(back(0))
    for_units(eng, nodes, own, 0)


def build(nc, x, src, dst, edge_attr, edge_weight, W_lin, Wf1, bf1, Wf2, bf2, Wm1, bm1, Wm2, bm2,
          W_up0, W_up1, mlp_w0, mlp_b0, mlp_w1, mlp_b1, mlp_w2, mlp_b2, W_out0, W_out1, out, ctx):
    nodes, chans = x.shape
    edges = src.shape[0]
    iterations = edges // (SLOTS * HALF)
    halves = iterations * SLOTS
    chunks = halves * HALF_CHUNKS
    pairs = halves // 2
    pair_chunks = PAIR // P
    tiles = -(-nodes // P)
    last_unit = -(-nodes // (UNIT_TILES * P)) - 1
    width = tiles * P + P
    all_windows = width // WINDOW
    assert chans == P and pairs <= P and all_windows % 2 == 0

    def sb(name, shape, dt=F32):
        return ctx.enter_context(nc.sbuf_tensor(name, shape, dt))

    def sem(name):
        return ctx.enter_context(nc.semaphore(name))

    def sems(name, n):
        return [sem(f"{name}{i}") for i in range(n)]

    h_dram = nc.dram_tensor("h_table", (nodes, P), F32).ap()
    v_dram = nc.dram_tensor("up_table", (nodes, P), F32).ap()
    near_dram = nc.dram_tensor("near_lengths", (halves, HALF), F32).ap()
    emb_dram = nc.dram_tensor("radial_embedding", (pairs, 2 * BESSEL, HALF), F32).ap()

    x_sb = sb("x_sb", [P, tiles, P])
    sums = sb("sums", [P, 2, width])
    scratch = sums[:, 1, :]
    windows_iota = sb("windows_iota", [P, all_windows * WINDOW], I16)
    iota = sb("iota", [P, WINDOW])
    ident = sb("ident", [P, P])
    ones = sb("ones", [P, 1])
    ones_bf = sb("ones_bf", [3, P], BF16)
    eps = sb("eps", [P, 1])
    exp_scale = sb("exp_scale", [P, 1])
    exp_bias = sb("exp_bias", [P, 1])
    is_radial, is_bessel = sb("is_radial", [P, 1]), sb("is_bessel", [P, 1])
    half_const = sb("half_const", [P, 1])

    W_lin_sb, W_linT = sb("W_lin_sb", [P, P]), sb("W_linT", [P, P])
    Wf1_sb = sb("Wf1_sb", [SPREAD + RADIAL, P])
    Wf2_sb, Wm1_sb, Wm2_sb = (sb(n, [P, P]) for n in ("Wf2_sb", "Wm1_sb", "Wm2_sb"))
    W_up_sb, W_outA, W_outB = (sb(n, [P, P]) for n in ("W_up_sb", "W_outA", "W_outB"))
    W_out_in = sb("W_out_in", [P, 2, MUL])
    w0_sb = sb("w0_sb", [2 * BESSEL, P])
    w1_sb = sb("w1_sb", [P, P])
    w2_sb = sb("w2_sb", [P, P])
    cols = sb("cols", [P, 6])
    bf1_c, bf1_s, bm1_c, bm1_s, b0_c, b1_c = (cols[:, i:i + 1] for i in range(6))
    brow = sb("brow", [1, 3, P])
    brest = sb("brest", [1, 3, P])
    bparts = sb("bparts", [1, 3, 3 * P], BF16)
    bias3 = sb("bias3", [3, 3, P], BF16)
    neg_centers = sb("neg_centers", [P, 1])

    dst_f = sb("dst_f", [pairs, PAIR])
    fits_row = sb("fits_row", [pairs, 1])
    sorted_flag = sb("sorted_flag", [1, 1], I32)
    srcT = sb("srcT", [P, pairs, pair_chunks])
    dstT = sb("dstT", [P, pairs, pair_chunks])
    relT = sb("relT", [P, pairs, pair_chunks])
    dirT = sb("dirT", [P, pairs, pair_chunks, 3])
    bases = sb("bases", [1, halves], I32)
    wt_space = sb("wt_space", [P, PAIR])
    wt_rows = wt_space[0:pairs, :]
    all_chunks = pairs * pair_chunks
    attr = scratch[0:pairs, 0:3 * PAIR]
    squares = scratch[:, 3 * PAIR:3 * PAIR + 3 * all_chunks]
    norm = wt_space[:, 0:all_chunks]
    assert 3 * PAIR + 3 * all_chunks <= width

    sent = sb("sent", [P, SLOTS, HALF_CHUNKS, P])
    picks = sb("picks", [P, 2, 2 * HALF_CHUNKS], I32)
    basis = sb("basis", [P, 2, HALF])
    soft = sb("soft", [P, 2, HALF])
    hid = sb("hid", [P, 2, HALF])
    src_i = sb("src_i", [pairs, PAIR], I32)
    dst_i = sb("dst_i", [pairs, PAIR], I32)
    msg = sb("msg", [P, 2, HALF_CHUNKS, 2 * P + MUL])
    dots = sb("dots", [P, 2, HALF_CHUNKS, 3, MUL])
    dot = sb("dot", [P, 2, HALF_CHUNKS, MUL])
    onehot = sb("onehot", [P, 2, HALF_CHUNKS, WINDOW])
    emb_in = sb("emb_in", [2 * BESSEL, 2, HALF])
    h1 = sb("h1", [P, 2, HALF])
    h2 = sb("h2", [P, 2, HALF])
    msg_flat = msg[:, :, :, :].rearrange("p a b c -> p (a b c)")
    src_f, rel2 = msg_flat[0:pairs, 0:PAIR], msg_flat[0:pairs, PAIR:2 * PAIR]
    rel_f = rel2.rearrange("g (a b) -> g a b", b=HALF)

    def rows_of(like):
        return like[0:pairs, :, :].rearrange("p a b -> p (a b)")
    fits, beyond = rows_of(soft), rows_of(hid)

    unit_in = sb("unit_in", [P, WIDE, UNIT_TILES, P])
    unit_T = sb("unit_T", [P, 2, UNIT_TILES * P])
    stage = sent[:, :, :, :].rearrange("p (s k) j c -> p s k (j c)", k=2)
    rows_out = [h[:, q, :].rearrange("p (t c) -> p t c", c=P) for h in (h1, h2) for q in range(2)]
    stats = sb("stats", [P, WIDE, UNIT_TILES, 6])
    mean_var = sb("mean_var", [P, WIDE, UNIT_TILES, 2])
    inverse = sb("inverse", [P, WIDE, UNIT_TILES])
    offset = sb("offset", [P, WIDE, UNIT_TILES])

    bank = [ctx.enter_context(nc.psum_tensor(f"bank{i}", [P, HALF], F32)) for i in range(8)]
    quads = [b[:, :].rearrange("p (j c) -> p j c", j=4) for b in bank]
    filtA = [bank[i] for i in (0, 1, 6, 7)]
    filtB = quads[2:4]
    winps = bank[4:6]
    outps = quads[2:6]

    s_const = sem("s_const")
    s_ident = sem("s_ident")
    s_gathering = sem("s_gathering")
    s_pool = sem("s_pool")
    d_rows = sems("d_rows", 4)
    s_near, d_near = sem("s_near"), sem("d_near")
    d_wlin, d_weights, d_bias = sem("d_wlin"), sem("d_weights"), sem("d_bias")
    d_x, d_bases, d_up = sem("d_x"), sem("d_bases"), sem("d_up")
    d_bparts = sem("d_bparts")
    s_blocks = sem("s_blocks")
    s_dve = sem("s_dve")
    s_own = sem("s_own")
    s_wT, s_wTc = sem("s_wT"), sem("s_wTc")
    s_turn, s_turned = sem("s_turn"), sem("s_turned")
    s_weights = sem("s_weights")
    s_flag, s_fits = sem("s_flag"), sem("s_fits")
    d_emb = sems("d_emb", 2)
    s_norm = sem("s_norm")

    def unit_sems(phase):
        by_dma = {k: sems(f"{phase}_{k}", WIDE) for k in ("loaded", "stored")}
        return by_dma | {k: sem(f"{phase}_{k}") for k in
                         ("normed", "turned", "copied", "product", "ready")}

    def dense_sems(phase):
        return {k: sem(f"{phase}_{k}") for k in
                ("staged", "first", "capped", "soft_e", "soft_l", "hidden", "second", "added")}

    table0, table1 = unit_sems("tab0"), unit_sems("tab1")
    dense0, dense1 = dense_sems("den0"), dense_sems("den1")
    s_out = sems("s_out", WIDE)
    s_zeroed = sem("s_zeroed")
    norm0, norm1 = ({k: sem(f"norm{n}_{k}") for k in
                     ("begun", "stats", "moments", "log", "inverse", "dve", "act")}
                    for n in range(2))

    def edge_sems(layer):
        by_dma = {"r_in": sems(f"L{layer}_r_in", 2), "landed": sems(f"L{layer}_landed", SLOTS)}
        own = (("squared", "basis", "capped", "exped", "logged", "soft"),
               ("act1", "filt2", "act2", "dots", "scaled", "dot"))[layer]
        return by_dma | {k: sem(f"L{layer}_{k}") for k in
                         ("picked", "filt1", "filt", "msg", "window", "added") + own}

    L0, L1 = edge_sems(0), edge_sems(1)
    every = [{k: sems(f"every{n}_{k}", 2) for k in ("onehot", "window", "added")} for n in range(2)]

    def stores_of(slot):
        return 16 * (1 + last_unit // WIDE + (slot <= last_unit % WIDE))

    def act_from(nm, u):
        return 1 if nm is norm0 else -(-u.tiles // 2)

    def row_tile(u, t):
        return x_sb[0:u.rows, at(u.tile(1, t), 1), :].rearrange("p a c -> p (a c)")

    block = ctx.enter_context(nc.Block())

    def at(start, size):
        return slice(start, start + size) if isinstance(start, int) else bass.ds(start, size)

    def by_chunk(tile_T, h):
        columns = tile_T[:, :, :].rearrange("p a b -> p (a b)")
        return columns[:, at(h.number(HALF_CHUNKS), HALF_CHUNKS)]

    @block.gpsimd
    def _(pool):
        g = nc.gpsimd
        g.memset(ident[:], 0.0).then_inc(s_pool, 1)
        pool.wait_ge(s_pool, 1)
        g.affine_select(out=ident[:], in_=ident[:], compare_op=ALU.not_equal, fill=1.0, base=0,
                        pattern=[[-1, P]], channel_multiplier=1).then_inc(s_ident, 1)
        made = [0]

        def constant(ins):
            made[0] += 1
            ins.then_inc(s_const, 1)
            pool.wait_ge(s_const, made[0])

        pool.wait_ge(s_ident, 1)
        constant(g.memset(ones[:], 1.0))
        constant(g.memset(ones_bf[:], 1.0))
        constant(g.memset(eps[:], LN_EPS))
        constant(g.memset(half_const[:], 0.5))
        constant(g.memset(basis[:], 0.0))
        for part in (neg_centers[0:SPREAD, :], neg_centers[SPREAD:P, :]):
            constant(g.iota(part, [[0, 1]], base=0, channel_multiplier=1,
                            allow_small_or_imprecise_dtypes=True))
        for row, n in ((iota, WINDOW), (windows_iota, all_windows * WINDOW)):
            constant(g.iota(row[:], [[1, n]], base=0, channel_multiplier=0,
                            allow_small_or_imprecise_dtypes=True))
        pool.dma_start(bases[:], dst.rearrange("(a n e) -> a n e", a=1, e=HALF)[:, :, 0],
                       allow_slow_non_contiguous=True).then_inc(d_bases, 16)
        for s in range(2):
            pool.dma_start(Wf1_sb[s * SPREAD:s * SPREAD + RADIAL, :], Wf1).then_inc(d_weights, 16)
        for w_sb, w in ((Wf2_sb, Wf2), (Wm1_sb, Wm1), (Wm2_sb, Wm2)):
            pool.dma_start(w_sb[:], w).then_inc(d_weights, 16)
        pool.dma_start(bf1_c, bf1.rearrange("(p a) -> p a", a=1)).then_inc(d_bias, 16)
        pool.dma_start(bm1_c, bm1.rearrange("(p a) -> p a", a=1)).then_inc(d_bias, 16)
        for s in range(2):
            pool.dma_start(b0_c[s * HIDDEN:(s + 1) * HIDDEN, :],
                         mlp_b0.rearrange("(p a) -> p a", a=1)).then_inc(d_bias, 16)
            pool.dma_start(b1_c[s * HIDDEN:(s + 1) * HIDDEN, :],
                         mlp_b1.rearrange("(p a) -> p a", a=1)).then_inc(d_bias, 16)
        for i, b in enumerate((bf2, bm2, mlp_b2)):
            pool.dma_start(brow[:, i, :], b.rearrange("(a c) -> a c", a=1)).then_inc(d_bias, 16)

        def table_stored(sm):
            for s in range(WIDE):
                pool.wait_ge(sm["stored"][s], stores_of(s))

        def gather(sm, table):
            def step(h):
                if h.parity == 0:
                    wait(pool, sm["picked"], h.pair_upto())
                wait(pool, sm["msg"], h.upto(SLOTS))
                pool.sem_inc(s_gathering, 1)
                for j in range(HALF_CHUNKS):
                    pick = picks[:, h.pair_slot, (h.parity) * HALF_CHUNKS + j:
                                 (h.parity) * HALF_CHUNKS + j + 1]
                    pool.indirect_dma_start(sent[:, h.slot, j, :], None, table,
                                            bass.IndirectOffsetOnAxis(pick, 0))\
                        .then_inc(sm["landed"][h.slot], 16)
            for_halves(pool, iterations, step, 0)

        table_stored(table0)
        gather(L0, h_dram)

        pool.wait_ge(dense0["first"], last_unit + 1)
        pool.wait_ge(s_norm, 2)
        g.memset(sums[:, :, :], 0.0).then_inc(s_zeroed, 1)
        table_stored(table1)
        gather(L1, v_dram)

    @block.sync
    def _(sp):
        sp.dma_start(src_i[:], src.rearrange("(g e) -> g e", e=PAIR)).then_inc(d_rows[0], 16)
        sp.dma_start(W_lin_sb[:], W_lin).then_inc(d_wlin, 16)

        def store_table(sm, table, u):
            wait(sp, sm["ready"], u.upto())
            rows = table[at(u.tile(P), u.cols), :]
            sp.dma_start(rows.rearrange("(t p) c -> p t c", p=u.rows),
                         rows_out[u.wide_slot][0:u.rows, 0:u.tiles, :])\
                .then_inc(sm["stored"][u.wide_slot], 16)

        def load_and_store(back):
            u, b = back(0), back(4)
            if u is not None:
                wait(sp, table0["turned"], u.upto(WIDE))
                rows = x[at(u.tile(P), u.cols), :]
                sp.dma_start(unit_in[0:u.rows, u.wide_slot, 0:u.tiles, :],
                             rows.rearrange("(t p) c -> p t c", p=u.rows))\
                    .then_inc(table0["loaded"][u.wide_slot], 16)
            if b is not None:
                store_table(table0, h_dram, b)
        for sm in (table0, table1):
            for s in range(WIDE):
                sp.sem_inc(sm["stored"][s], 16)
        for_units(sp, nodes, load_and_store, 4)

        sp.wait_ge(s_near, 1)
        sp.dma_start(near_dram.rearrange("(g a) e -> g (a e)", a=2), wt_rows).then_inc(d_near, 16)
        sp.wait_ge(s_weights, 1)
        for part in range(3):
            sp.dma_start(bias3[part:part + 1, :, :], bparts[:, part, :])\
                .then_inc(d_bparts, 16)

        wt_halves = edge_weight.rearrange("(n e) -> n e", e=HALF)

        whole = nodes // P
        assert whole % FEATURE_LOADS == 0

        def load_features(piece):
            n = whole // FEATURE_LOADS
            some = slice(piece * n, (piece + 1) * n)
            rows = x[some.start * P:some.stop * P, :].rearrange("(t p) c -> p t c", p=P)
            sp.dma_start(x_sb[:, some, :], rows).then_inc(d_x, 16)
            if piece == 0 and nodes % P:
                sp.dma_start(x_sb[0:nodes % P, whole, :], x[whole * P:nodes, :]).then_inc(d_x, 16)

        def load_layer1_weights():
            sp.wait_ge(s_blocks, 1)
            for s in range(2):
                own = slice(s * HIDDEN, (s + 1) * HIDDEN)
                sp.dma_start(w0_sb[s * BESSEL:(s + 1) * BESSEL, own], mlp_w0).then_inc(d_up, 16)
                sp.dma_start(w1_sb[own, own], mlp_w1).then_inc(d_up, 16)
                sp.dma_start(w2_sb[own, :], mlp_w2).then_inc(d_up, 16)
            sp.dma_start(W_up_sb[0:MUL, 0:MUL], W_up0).then_inc(d_up, 16)
            for c in range(3):
                cs = slice(MUL * (c + 1), MUL * (c + 2))
                sp.dma_start(W_up_sb[MUL + c:P:3, cs], W_up1).then_inc(d_up, 16)
                sp.dma_start(W_out_in[cs, 0, :], W_out1[MUL:2 * MUL, :]).then_inc(d_up, 16)
                sp.dma_start(W_out_in[cs, 1, :], W_out1[0:MUL, :]).then_inc(d_up, 16)
            sp.dma_start(W_out_in[0:MUL, 0, :], W_out0[0:MUL, :]).then_inc(d_up, 16)
            sp.dma_start(W_out_in[0:MUL, 1, :], W_out0[MUL:2 * MUL, :]).then_inc(d_up, 16)

        def move_basis(h):
            if h.parity:
                return
            g = h.pair_slot
            b = h.before(2)
            pair_b = b.pair()
            read, stored = h.upto(3), h.uses(32, 1)
            if h.real():
                wait(sp, d_emb[g], stored)
                wait(sp, L0["filt1"], read)
                for s in range(2):
                    first = s * SPREAD
                    sp.dma_start(basis[first:first + RADIAL, g, :],
                                 wt_halves[at(h.number(1, s), 1), :].broadcast_to([RADIAL, HALF]))\
                        .then_inc(L0["r_in"][g], 16)
                    sp.dma_start(basis[first + RADIAL:first + ROWS, g, :],
                                 near_dram[at(h.number(1, s), 1), :].broadcast_to([BESSEL, HALF]))\
                        .then_inc(L0["r_in"][g], 16)
            if b.real():
                g = b.pair_slot
                wait(sp, L0["basis"], b.pair_upto())
                for s in range(2):
                    sp.dma_start(emb_dram[at(pair_b, 1), s * BESSEL:(s + 1) * BESSEL, :]
                                 .rearrange("a k e -> (a k) e"),
                                 basis[s * SPREAD + RADIAL:s * SPREAD + ROWS, g, :])\
                        .then_inc(d_emb[g], 16)
            if h.counter.eng is None and h.pair() < FEATURE_LOADS:
                load_features(h.pair())
                if h.pair() == FEATURE_LOADS - 1:
                    load_layer1_weights()
        sp.wait_ge(s_const, 9)
        sp.wait_ge(d_near, 16)
        for_halves(sp, iterations, move_basis, 2)

        def load_embedding(h):
            if h.parity:
                return
            g = h.pair_slot
            wait(sp, L1["filt1"], h.pair_upto(2))
            sp.dma_start(emb_in[:, g, :],
                         emb_dram[at(h.pair(), 1), :, :].rearrange("a k e -> (a k) e"))\
                .then_inc(L1["r_in"][g], 16)
        each_unit(sp, nodes, lambda u: store_table(table1, v_dram, u))
        for s in range(2):
            sp.wait_ge(d_emb[s], 32 * iterations)
        for_halves(sp, iterations, load_embedding, 0)

        def store_out(back):
            u = back(0)
            if u is None:
                return
            for by in ("dve", "act"):
                wait(sp, norm1[by], u.upto(-WIDE))
            rows = out[at(u.tile(P), u.cols), :]
            sp.dma_start(rows.rearrange("(t p) c -> p t c", p=u.rows),
                         rows_out[u.wide_slot][0:u.rows, 0:u.tiles, :])\
                .then_inc(s_out[u.wide_slot], 16)
        for s in range(WIDE):
            sp.sem_inc(s_out[s], 16)
        for_units(sp, nodes, store_out, 0)
        for s in range(WIDE):
            sp.wait_ge(s_out[s], stores_of(s))

    @block.scalar
    def _(act):
        a = nc.scalar
        act.dma_start(dst_i[:], dst.rearrange("(g e) -> g e", e=PAIR)).then_inc(d_rows[1], 16)
        act.dma_start(attr, edge_attr.rearrange("(g e) c -> g (e c)", e=PAIR))\
            .then_inc(d_rows[3], 16)
        act.dma_start(wt_rows, edge_weight.rearrange("(g e) -> g e", e=PAIR))\
            .then_inc(d_rows[2], 16)
        act.wait_ge(s_wT, 1)
        a.activation(W_linT[:], bank[6][:, 0:P], ACT.Copy).then_inc(s_wTc, 1)

        def copy_tables(sm, scale):
            def step(back):
                u, b = back(0), back(2)
                if u is not None:
                    wait(act, sm["turned"], u.upto())
                    wait(act, sm["product"], u.upto(2))
                    a.activation(unit_T[:, u.slot, 0:u.cols], bank[u.slot][:, 0:u.cols], ACT.Copy)\
                        .then_inc(sm["copied"], 1)
                if b is not None:
                    wait(act, sm["product"], b.upto())
                    wait(act, sm["stored"][b.wide_slot], b.uses(16))
                    rows_b = rows_out[b.wide_slot][0:b.rows, 0:b.tiles, :]
                    a.activation(rows_b, quads[2 + b.slot][0:b.rows, 0:b.tiles, :], ACT.Copy,
                                 scale=scale).then_inc(sm["ready"], 1)
            for_units(act, nodes, step, 2)

        copy_tables(table0, 1.0)

        def pick(sm, h):
            for s in range(2):
                wait(act, sm["landed"][h.slot + s], h.uses(64, 1))
            senders = srcT[:, :, :].rearrange("p a b -> p (a b)")
            a.activation(picks[:, h.pair_slot, :],
                         senders[:, at(h.number(HALF_CHUNKS), 2 * HALF_CHUNKS)], ACT.Copy)\
                .then_inc(sm["picked"], 1)

        act.wait_ge(s_turned, 2)
        for n in range(0, SLOTS, 2):
            pick(L0, Half(n, halves))
        a.preload_act_table_set("natural_log_exp_and_others")

        def make_basis(h):
            g = h.pair_slot
            used = slice(0, SPREAD + ROWS)
            rows = basis[used, g, :]
            wait(act, L0["r_in"][g], h.uses(64))
            a.activation(rows, rows, ACT.Square, bias=neg_centers[used, :])\
                .then_inc(L0["squared"], 1)
            wait(act, L0["squared"], h.pair_upto())
            a.activation(rows, rows, ACT.Exp, scale=exp_scale[used, :], bias=exp_bias[used, :])\
                .then_inc(L0["basis"], 1)

        def soft_log(sm, parity, n, cols_n, use):
            wait(act, sm["capped"], use)
            tile_ = soft[:, parity, 0:cols_n]
            a.activation(tile_, tile_, ACT.Exp).then_inc(sm[n[0]], 1)
            wait(act, sm[n[0]], use)
            a.activation(tile_, tile_, ACT.Ln, scale=0.5, bias=half_const[:, :])\
                .then_inc(sm[n[1]], 1)

        def layer0(h):
            if h.parity == 0 and h.real():
                if h.counter.eng is not None or h.rel >= SLOTS:
                    pick(L0, h)
                make_basis(h)
            b = h.before(2)
            if b.real():
                soft_log(L0, b.parity, ("exped", "logged"), HALF, b.upto())
            if h.counter.eng is None and h.rel == 7:
                act.wait_ge(s_norm, 2)
                a.activation(norm, norm, ACT.Sqrt).then_inc(s_norm, 1)
                a.preload_act_table_set("natural_log_exp_and_others")
        act.wait_ge(s_weights, 1)
        for_halves(act, iterations, layer0, 2)

        for nm in (norm0, norm1):
            act.sem_inc(nm["act"], WIDE)

        def root(nm, u):
            rows, w, q = slice(0, u.rows), u.wide_slot, slice(0, u.tiles)
            wait(act, nm["moments"], u.upto())
            a.activation(inverse[rows, w, q], mean_var[rows, w, q, 1], ACT.Ln, bias=eps[rows, :])\
                .then_inc(nm["log"], 1)
            wait(act, nm["log"], u.upto())
            a.activation(inverse[rows, w, q], inverse[rows, w, q], ACT.Exp, scale=-0.5)\
                .then_inc(nm["inverse"], 1)

        def normalise(nm, u, source, target):
            rows, w = slice(0, u.rows), u.wide_slot
            for t in range(act_from(nm, u), u.tiles):
                last = a.activation(target(t), source[rows, t, :], ACT.Identity,
                                    scale=inverse[rows, w, t:t + 1], bias=offset[rows, w, t:t + 1])
            if act_from(nm, u) < u.tiles:
                last.then_inc(nm["act"], 1)
            else:
                wait(act, nm["act"], u.upto(1 - WIDE))
                act.sem_inc(nm["act"], 1)

        def dense(back):
            u, f, r = back(0), back(4), back(3)
            if u is not None:
                soft_log(dense0, u.slot, ("soft_e", "soft_l"), u.cols, u.upto())
            if f is not None:
                wait(act, norm0["dve"], f.upto(-WIDE))
                normalise(norm0, f, outps[f.wide_slot], lambda t: row_tile(f, t))
            if r is not None:
                root(norm0, r)
        for_units(act, nodes, dense, 4)
        copy_tables(table1, 1.0 / math.sqrt(MUL))
        for s in range(WIDE):
            act.wait_ge(table1["stored"][s], stores_of(s))

        def layer1(h):
            if h.parity == 0 and h.real():
                pick(L1, h)
                g = h.pair_slot
                wait(act, L1["filt1"], h.pair_upto())
                wait(act, L1["filt2"], h.pair_upto(2))
                a.activation(h1[:, g, :], bank[0][:], ACT.Silu, bias=b0_c).then_inc(L1["act1"], 1)
            if h.parity == 1:
                b = h.before(1)
                if b.real():
                    g = b.pair_slot
                    wait(act, L1["filt2"], b.pair_upto())
                    wait(act, L1["filt"], b.upto(3))
                    a.activation(h2[:, g, :], bank[1][:], ACT.Silu, bias=b1_c)\
                        .then_inc(L1["act2"], 1)
        for_halves(act, iterations, layer1, 0)

        def finish(back):
            u, r, f = back(0), back(2), back(3)
            if u is not None:
                wait(act, dense1["second"], u.upto(2))
                n = u.cols
                a.activation(stage[:, u.slot, :, 0:n], sums[:, :, at(u.tile(P), n)], ACT.Copy)\
                    .then_inc(dense1["staged"], 1)
            if r is not None:
                root(norm1, r)
            if f is not None:
                wait(act, norm1["dve"], f.upto(-WIDE))
                wait(act, s_out[f.wide_slot], f.uses(16))
                normalise(norm1, f, outps[f.wide_slot],
                          lambda t: rows_out[f.wide_slot][0:f.rows, t, :])
        a.preload_act_table_set("natural_log_exp_and_others")
        act.wait_ge(L1["added"], halves)
        for_units(act, nodes, finish, 3)

    @block.tensor
    def _(pe):
        t_ = nc.tensor
        pe.wait_ge(s_ident, 1)
        pe.wait_ge(d_wlin, 16)
        t_.transpose(bank[6][:, 0:P], W_lin_sb[:], ident[:]).then_inc(s_wT, 1)

        turns = [0]

        def turn_rows(rows):
            if turns[0] >= 2:
                pe.wait_ge(s_turned, turns[0] - 1)
            for j, r in enumerate(rows):
                last = t_.transpose(quads[6 + turns[0] % 2][:, j, 0:pairs], r,
                                    ident[0:pairs, 0:pairs])
            last.then_inc(s_turn, 1)
            turns[0] += 1

        def turn_all(tile_rows):
            for j in range(0, pair_chunks, 4):
                turn_rows([tile_rows[:, (j + i) * P:(j + i + 1) * P] for i in range(4)])

        pe.wait_ge(s_wTc, 1)
        pe.wait_ge(s_dve, 1)
        turn_all(src_f)

        def turn_unit(sm, u):
            if sm is table0:
                wait(pe, sm["loaded"][u.wide_slot], u.uses(16))
            else:
                wait(pe, sm["normed"], u.upto())
            wait(pe, sm["copied"], u.upto(2))
            for t in range(u.tiles):
                last = t_.transpose(bank[u.slot][:, t * P:t * P + u.rows],
                                    unit_in[0:u.rows, u.wide_slot, t, :], ident[0:u.rows, 0:u.rows])
            last.then_inc(sm["turned"], 1)

        def product_unit(sm, u, weight):
            wait(pe, sm["copied"], u.upto())
            wait(pe, sm["ready"], u.upto(2))
            for t in range(u.tiles):
                last = t_.matmul(quads[2 + u.slot][0:u.rows, t, :],
                                 unit_T[:, u.slot, t * P:t * P + u.rows], weight[:],
                                 start=True, stop=True)
            last.then_inc(sm["product"], 1)

        def tables(sm, weight):
            def step(back):
                if back(0) is not None:
                    turn_unit(sm, back(0))
                if back(1) is not None:
                    product_unit(sm, back(1), weight)
            for_units(pe, nodes, step, 1)

        tables(table0, W_linT)

        pe.wait_ge(s_dve, 2)
        turn_all(dst_f[:, :])
        pe.wait_ge(d_rows[3], 16)
        for c in range(3):
            turn_rows([attr[:, j * P * 3 + c:((j + 1) * P - 1) * 3 + c + 1:3] for j in range(4)])
            turn_rows([attr[:, j * P * 3 + c:((j + 1) * P - 1) * 3 + c + 1:3] for j in range(4, 8)])
        pe.wait_ge(s_dve, 3)
        turn_all(rel2)
        pe.wait_ge(s_fits, 1)
        pe.wait_ge(s_const, 1)
        pe.wait_ge(s_turned, 12)
        t_.matmul(bank[6][0:1, 0:1], fits_row[:], ones[0:pairs, :], start=True, stop=True)\
            .then_inc(s_flag, 1)

        def products(out_bank, n_tiles, rows, lhs, weight, which):
            for j in range(n_tiles):
                t_.matmul(out_bank[0:rows, j, :], lhs(j), weight, start=(j == 0), stop=False,
                          skip_group_check=True)
            return t_.matmul(out_bank[0:rows, 0:n_tiles, :], ones_bf[:, 0:rows],
                             bias3[:, which:which + 1, :].broadcast_to([3, n_tiles, P]),
                             start=False, stop=True, skip_group_check=True)

        def window_sums(sm, h, outputs):
            p = h.parity
            wait(pe, sm["msg"], h.upto())
            b = h.before(2)
            wait(pe, sm["added"], b.upto())
            ps = winps[p][:, :].rearrange("p (k n) -> p k n", n=WINDOW)
            for k in range(outputs):
                for j in range(HALF_CHUNKS):
                    last = t_.matmul(ps[:, k, :], msg[:, p, j, k * P:(k + 1) * P],
                                     onehot[:, p, j, :], start=(j == 0),
                                     stop=(j == HALF_CHUNKS - 1))
            last.then_inc(sm["window"], 1)

        def every_window(sm, ev, h, outputs):
            p = h.parity
            first = h.number(all_windows // 2)
            with pe.Fori(1, all_windows // 2 + 1) as i:
                use = pe.snap(i + first)
                wait(pe, sm["msg"], h.upto())
                for q in range(2):
                    ps = winps[q][:, :].rearrange("p (k n) -> p k n", n=WINDOW)
                    pe.wait_ge(ev["onehot"][q], use)
                    pe.wait_ge(ev["added"][q], use)
                    for k in range(outputs):
                        for j in range(HALF_CHUNKS):
                            last = t_.matmul(ps[:, k, :], msg[:, p, j, k * P:(k + 1) * P],
                                             onehot[:, q, j, :], start=(j == 0),
                                             stop=(j == HALF_CHUNKS - 1))
                    last.then_inc(ev["window"][q], 1)

        def hidden0(h):
            p, g = h.parity, h.pair_slot
            b = h.before(SLOTS)
            wait(pe, L0["basis"], h.pair_upto())
            wait(pe, L0["soft"], b.upto())
            rows = slice(p * SPREAD, p * SPREAD + RADIAL)
            t_.matmul(filtA[h.slot][:, :], Wf1_sb[rows, :], basis[rows, g, :],
                      start=True, stop=True).then_inc(L0["filt1"], 1)

        def filter0(h):
            p = h.parity
            b = h.before(2)
            wait(pe, L0["msg"], b.upto())
            wait(pe, L0["soft"], h.upto())
            products(filtB[p], HALF_CHUNKS, P, lambda j: hid[:, p, j * P:(j + 1) * P],
                     Wf2_sb[:], 0).then_inc(L0["filt"], 1)

        def hidden1(h):
            g = h.pair_slot
            wait(pe, L1["r_in"][g], h.uses(16))
            b = h.before(2)
            wait(pe, L1["act1"], b.pair_upto())
            t_.matmul(bank[0][:, :], w0_sb[:], emb_in[:, g, :], start=True, stop=True)\
                .then_inc(L1["filt1"], 1)

        def second1(h):
            g = h.pair_slot
            wait(pe, L1["act1"], h.pair_upto())
            b = h.before(2)
            wait(pe, L1["act2"], b.pair_upto())
            t_.matmul(bank[1][:, :], w1_sb[:], h1[:, g, :], start=True, stop=True)\
                .then_inc(L1["filt2"], 1)

        def filter1(h):
            p, g = h.parity, h.pair_slot
            b = h.before(2)
            wait(pe, L1["msg"], b.upto())
            wait(pe, L1["act2"], h.pair_upto())
            rows = slice(p * HIDDEN, (p + 1) * HIDDEN)
            products(filtB[p], HALF_CHUNKS, P, lambda j: h2[rows, g, j * P:(j + 1) * P],
                     w2_sb[rows, :], 2).then_inc(L1["filt"], 1)

        def layer0(h):
            if h.real():
                hidden0(h)
            b = h.before(3)
            if b.real():
                filter0(b)
            b = h.before(5)
            if b.real():
                window_sums(L0, b, 1)

        def layer1(h):
            if h.parity == 0 and h.real():
                hidden1(h)
            b = h.before(1)
            if h.parity == 1 and b.real():
                second1(b)
            b = h.before(3)
            if b.real():
                filter1(b)
            b = h.before(5)
            if b.real():
                window_sums(L1, b, 2)

        def layer0_any(h):
            hidden0(h)
            filter0(h)
            every_window(L0, every[0], h, 1)

        def layer1_any(h):
            if h.parity == 0:
                hidden1(h)
                second1(h)
            filter1(h)
            every_window(L1, every[1], h, 2)

        def tables_read(sm):
            pe.wait_ge(sm["ready"], last_unit + 1)
        tables_read(table0)
        pe.wait_ge(d_weights, 16 * 5)
        pe.wait_ge(d_bparts, 48)
        pe.wait_ge(s_flag, 2)
        flag = pe.value_load(sorted_flag[0:1, 0:1], min_val=0, max_val=1)
        with pe.If(flag):
            for_halves(pe, iterations, layer0, 5)
        with pe.Else():
            for_halves(pe, iterations, layer0_any, 0)

        def dense_first(u):
            n = u.cols
            wait(pe, dense0["hidden"], u.upto(2))
            t_.matmul(filtA[u.slot][:, 0:n], Wm1_sb[:], sums[:, 0, at(u.tile(P), n)],
                      start=True, stop=True).then_inc(dense0["first"], 1)

        def dense_second(u):
            wait(pe, norm0["dve"], u.upto())
            wait(pe, norm0["act"], u.upto())
            wait(pe, dense0["hidden"], u.upto())
            products(outps[u.wide_slot], u.tiles, u.rows,
                     lambda t: hid[:, u.slot, t * P:t * P + u.rows], Wm2_sb[:], 1)\
                .then_inc(dense0["second"], 1)
            t_.matmul(outps[u.wide_slot][0:u.rows, 0:u.tiles, :], ident[0:u.rows, 0:u.rows],
                      x_sb[0:u.rows, at(u.tile(), u.tiles), :], start=False, stop=True,
                      skip_group_check=True).then_inc(dense0["added"], 1)

        def dense(back):
            if back(0) is not None:
                dense_first(back(0))
            if back(2) is not None:
                dense_second(back(2))
        pe.wait_ge(d_x, 16 * (FEATURE_LOADS + bool(nodes % P)))
        pe.wait_ge(L0["added"], halves)
        for_units(pe, nodes, dense, 2)
        pe.wait_ge(d_up, 16 * 18)
        tables(table1, W_up_sb)
        tables_read(table1)
        flag = pe.value_load(sorted_flag[0:1, 0:1], min_val=0, max_val=1)
        with pe.If(flag):
            for_halves(pe, iterations, layer1, 5)
        with pe.Else():
            for_halves(pe, iterations, layer1_any, 0)

        def outputs(back):
            u = back(0)
            if u is None:
                return
            wait(pe, dense1["staged"], u.upto())
            wait(pe, norm1["dve"], u.upto())
            wait(pe, norm1["act"], u.upto())
            for t in range(u.tiles):
                for k, w in enumerate((W_outA, W_outB)):
                    last = t_.matmul(outps[u.wide_slot][0:u.rows, t, :],
                                     stage[:, u.slot, k, t * P:t * P + u.rows], w[:],
                                     start=(t == k == 0), stop=False, skip_group_check=True)
            last.then_inc(dense1["second"], 1)
            t_.matmul(outps[u.wide_slot][0:u.rows, 0:u.tiles, :], ident[0:u.rows, 0:u.rows],
                      x_sb[0:u.rows, at(u.tile(), u.tiles), :], start=False, stop=True,
                      skip_group_check=True).then_inc(dense1["added"], 1)
        pe.wait_ge(s_weights, 2)
        for_units(pe, nodes, outputs, 0)

    @block.vector
    def _(dve):
        v = nc.vector
        steps = [0]

        def then(ins):
            steps[0] += 1
            ins.then_inc(s_own, 1)
            dve.wait_ge(s_own, steps[0])

        turned = [0]

        def copy_turn(tile_T):
            for j in (0, 4):
                turned[0] += 1
                dve.wait_ge(s_turn, turned[0])
                v.tensor_copy(tile_T[:, :, j:j + 4].rearrange("p g j -> p j g"),
                              quads[6 + (turned[0] - 1) % 2][:, :, 0:pairs]).then_inc(s_turned, 1)

        for w_sb in (w0_sb, w1_sb, W_up_sb, W_outA, W_outB):
            last = v.memset(w_sb[:], 0.0)
        last.then_inc(s_blocks, 1)
        dve.wait_ge(d_rows[0], 16)
        v.tensor_copy(src_f, src_i[:]).then_inc(s_dve, 1)
        dve.wait_ge(d_rows[1], 16)
        v.tensor_copy(dst_f[:], dst_i[:]).then_inc(s_dve, 1)
        copy_turn(srcT)
        dve.wait_ge(s_dve, 2)
        d3 = dst_f[:, :].rearrange("g (a b) -> g a b", b=HALF)
        v.tensor_tensor(rel_f, d3, d3[:, :, 0:1].broadcast_to([pairs, 2, HALF]),
                        ALU.subtract).then_inc(s_dve, 1)
        dve.wait_ge(d_rows[2], 16)
        then(v.tensor_scalar(beyond, wt_rows, 1.0, FAR, ALU.is_gt, ALU.mult))
        v.scalar_tensor_tensor(out=wt_rows, in0=wt_rows, scalar=0.0, in1=beyond, op0=ALU.max,
                               op1=ALU.add).then_inc(s_near, 1)
        then(v.tensor_scalar(fits, rel2, 0.0, None, ALU.is_ge))
        then(v.scalar_tensor_tensor(out=fits, in0=rel2, scalar=float(WINDOW), in1=fits,
                                    op0=ALU.is_lt, op1=ALU.mult))
        then(v.scalar_tensor_tensor(out=fits, in0=dst_f[:], scalar=float(nodes), in1=fits,
                                    op0=ALU.is_ge, op1=ALU.max))
        v.tensor_reduce(fits_row[:], fits, AXES.X, ALU.min).then_inc(s_fits, 1)

        then(v.memset(sums[:, 0, :], 0.0))
        dve.wait_ge(s_const, 9)
        delta = np.float32(CUTOFF) / np.float32(RADIAL - 1)
        number = neg_centers
        then(v.tensor_scalar(is_radial[:], number[:], float(RADIAL), None, ALU.is_lt))
        then(v.tensor_scalar(is_bessel[:], number[:], float(RADIAL), None, ALU.is_ge))
        then(v.tensor_scalar(exp_bias[:], number[:], -float(RADIAL), -1.0 / (BESSEL - 1), ALU.add,
                             ALU.mult))
        then(v.tensor_tensor(exp_bias[:], exp_bias[:], is_bessel[:], ALU.mult))
        then(v.scalar_tensor_tensor(out=number[:], in0=number[:], scalar=-float(delta),
                                    in1=is_radial[:], op0=ALU.mult, op1=ALU.mult))
        then(v.tensor_tensor(neg_centers[:], number[:], exp_bias[:], ALU.add))
        then(v.tensor_scalar(exp_bias[:], is_bessel[:], 0.5 * math.log(BESSEL), None, ALU.mult))
        then(v.tensor_scalar(exp_scale[:], is_radial[:], -float(1.0 / (2.0 * delta * delta)), None,
                             ALU.mult))
        then(v.scalar_tensor_tensor(out=exp_scale[:], in0=is_bessel[:],
                                    scalar=-0.5 * (BESSEL - 1) ** 2, in1=exp_scale[:],
                                    op0=ALU.mult, op1=ALU.add))
        dve.wait_ge(d_bias, 16 * 9)
        then(v.tensor_scalar(bf1_s, bf1_c, -math.log(2.0), None, ALU.add))
        then(v.tensor_scalar(bm1_s, bm1_c, -math.log(2.0), None, ALU.add))
        b_all = brow[:, :, :].rearrange("a b c -> a (b c)")
        r_all = brest[:, :, :].rearrange("a b c -> a (b c)")
        then(v.tensor_copy(bparts[:, 0, :], b_all))
        then(v.tensor_tensor(r_all, b_all, bparts[:, 0, :], ALU.subtract))
        then(v.tensor_copy(bparts[:, 1, :], r_all))
        then(v.tensor_tensor(r_all, r_all, bparts[:, 1, :], ALU.subtract))
        v.tensor_copy(bparts[:, 2, :], r_all).then_inc(s_weights, 1)
        copy_turn(dstT)
        for c in range(3):
            copy_turn(dirT[:, :, :, c])
        copy_turn(relT)
        dve.wait_ge(s_flag, 1)
        v.tensor_scalar(sorted_flag[:], bank[6][0:1, 0:1], pairs - 0.5, None, ALU.is_ge)\
            .then_inc(s_flag, 1)

        def one_hots(h, sm):
            p = h.parity
            b = h.before(2)
            wait(dve, sm["window"], b.upto())
            v.tensor_tensor(onehot[:, p],
                            by_chunk(relT, h).rearrange("p (j a) -> p j a", a=1)
                            .broadcast_to([P, HALF_CHUNKS, WINDOW]),
                            iota[:, :].rearrange("p (a n) -> p a n", a=1)
                            .broadcast_to([P, HALF_CHUNKS, WINDOW]), ALU.is_equal)

        def add_window(sm, h, outputs, base):
            ps = winps[h.parity][:, :].rearrange("p (k n) -> p k n", n=WINDOW)
            wait(dve, sm["window"], h.upto())
            b = h.before(1)
            wait(dve, sm["added"], b.upto())
            here = sums[:, 0:outputs, at(base, WINDOW)]
            v.tensor_tensor(here, here, ps[:, 0:outputs, :], ALU.add).then_inc(sm["added"], 1)

        def cap0(h):
            p = h.parity
            b = h.before(2)
            wait(dve, L0["soft"], b.upto())
            wait(dve, L0["filt1"], h.upto())
            v.tensor_scalar(soft[:, p, :], filtA[h.slot][:, :], bf1_c, EXP_CAP, ALU.add, ALU.min)\
                .then_inc(L0["capped"], 1)

        def soft0(h):
            p = h.parity
            b = h.before(2)
            wait(dve, L0["filt"], b.upto())
            wait(dve, L0["logged"], h.upto())
            v.scalar_tensor_tensor(out=hid[:, p, :], in0=filtA[h.slot][:, :], scalar=bf1_s,
                                   in1=soft[:, p, :], op0=ALU.add, op1=ALU.max)\
                .then_inc(L0["soft"], 1)

        def msg0(h):
            p = h.parity
            wait(dve, L0["filt"], h.upto())
            wait(dve, L0["landed"][h.slot], h.uses(64))
            b = h.before(2)
            wait(dve, L0["window"], b.upto())
            v.tensor_tensor(msg[:, p, :, 0:P], filtB[p], sent[:, h.slot], ALU.mult)\
                .then_inc(L0["msg"], 1)

        def msg1(h):
            p = h.parity
            filt = filtB[p].rearrange("p j (i m) -> p j i m", m=MUL)
            rows = sent[:, h.slot]
            vec = rows[:, :, MUL:].rearrange("p j (c m) -> p j c m", m=MUL)
            cube = [P, HALF_CHUNKS, 3, MUL]
            dirs = dirT[:, :, :, :].rearrange("p a b c -> p (a b) c")
            dirs = dirs[:, at(h.number(HALF_CHUNKS), HALF_CHUNKS), :]\
                .rearrange("p j (c m) -> p j c m", m=1).broadcast_to(cube)
            wait(dve, L1["landed"][h.slot], h.uses(64))
            v.tensor_tensor(dots[:, p], vec, dirs, ALU.mult).then_inc(L1["dots"], 1)
            wait(dve, L1["filt"], h.upto())
            b = h.before(2)
            wait(dve, L1["window"], b.upto())
            scaled = msg[:, p, :, :].rearrange("p j (q m) -> p j q m", m=MUL)[:, :, 0:9:8, :]
            v.tensor_tensor(scaled, filt[:, :, 0:2, :],
                            rows[:, :, 0:MUL].rearrange("p j (a m) -> p j a m", a=1)
                            .broadcast_to([P, HALF_CHUNKS, 2, MUL]), ALU.mult)\
                .then_inc(L1["scaled"], 1)
            wait(dve, L1["dots"], h.upto())
            v.tensor_reduce(dot[:, p], dots[:, p].rearrange("p j c m -> p j m c"), AXES.X, ALU.add)\
                .then_inc(L1["dot"], 1)
            v.tensor_tensor(msg[:, p, :, MUL:P].rearrange("p j (c m) -> p j c m", m=MUL), vec,
                            filt[:, :, 2:3, :].broadcast_to(cube), ALU.mult)
            wait(dve, L1["scaled"], h.upto())
            v.tensor_tensor(msg[:, p, :, P + MUL:2 * P].rearrange("p j (c m) -> p j c m", m=MUL),
                            msg[:, p, :, 2 * P:].rearrange("p j (a m) -> p j a m", a=1)
                            .broadcast_to(cube), dirs, ALU.mult)
            wait(dve, L1["dot"], h.upto())
            v.tensor_tensor(msg[:, p, :, P:P + MUL], filt[:, :, 3, :], dot[:, p], ALU.mult)\
                .then_inc(L1["msg"], 1)

        def loop_layer(step, lag):
            def load_bases(first, n):
                if n <= 0:
                    return []
                _, values = nc.values_load_multi_w_load_instructions(
                    bases[0:1, at(first, n)], engines=[mybir.EngineType.DVE], min_val=0,
                    max_val=width - WINDOW, skip_runtime_bounds_check_because="receivers are nodes")
                return values
            count = iterations * SLOTS
            peeled = min(2, iterations)

            def steps_of(halves_, first, values):
                for i, h in enumerate(halves_):
                    step(h, values[i + first] if i + first >= 0 else None)

            for it in range(peeled):
                first = it * SLOTS - lag
                values = load_bases(max(first, 0), first + SLOTS - max(first, 0))
                steps_of([Half(it * SLOTS + s, count) for s in range(SLOTS)], min(first, 0), values)
            if iterations > peeled:
                with dve.Fori(peeled, iterations) as it:
                    counter = Counter(dve, it)
                    values = load_bases(counter.value(SLOTS, -lag), SLOTS)
                    steps_of([Half(s, count, counter) for s in range(SLOTS)], 0, values)
            values = load_bases(count - lag, lag)
            steps_of([Half(n, count) for n in range(count, count + lag)], 0, values)

        raw = dirT[:, :, :, :].rearrange("p g j c -> p (g j c)")

        def squared_lengths(part):
            if part == 0:
                dve.wait_ge(s_turned, 12)
                v.tensor_tensor(squares, raw, raw, ALU.mult).then_inc(s_norm, 1)
            else:
                dve.wait_ge(d_near, 16)
                dve.wait_ge(s_norm, 1)
                v.tensor_reduce(norm, squares.rearrange("p (e c) -> p e c", c=3), AXES.X, ALU.add)\
                    .then_inc(s_norm, 1)

        def layer0(h, base):
            if h.counter.eng is None and h.rel in (5, 6):
                squared_lengths(h.rel - 5)
            b1, b2, b4, b6 = (h.before(i) for i in (1, 2, 4, 6))
            if b1.real():
                cap0(b1)
            if b4.real():
                one_hots(b4, L0)
                msg0(b4)
            if b6.real():
                add_window(L0, b6, 1, base)
            if b2.real():
                soft0(b2)

        def layer1(h, base):
            b4, b6 = h.before(4), h.before(6)
            if b6.real():
                add_window(L1, b6, 2, base)
            if b4.real():
                one_hots(b4, L1)
                msg1(b4)

        def every_window(sm, ev, h, outputs):
            first = h.number(all_windows // 2)
            targets = by_chunk(dstT, h)

            def hots(i, q):
                lo = i * (2 * WINDOW) + (q - 2) * WINDOW
                v.tensor_tensor(onehot[:, q],
                                targets.rearrange("p (j a) -> p j a", a=1)
                                .broadcast_to([P, HALF_CHUNKS, WINDOW]),
                                windows_iota[:, bass.ds(lo, WINDOW)]
                                .rearrange("p (a n) -> p a n", a=1)
                                .broadcast_to([P, HALF_CHUNKS, WINDOW]), ALU.is_equal)\
                    .then_inc(ev["onehot"][q], 1)

            with dve.Fori(1, all_windows // 2 + 1) as i:
                use = dve.snap(i + first)
                more = dve.snap(use + 1)
                for q in range(2):
                    dve.wait_ge(ev["window"][q], use)
                    hots(i, q)
                for q in range(2):
                    ps = winps[q][:, :].rearrange("p (k n) -> p k n", n=WINDOW)
                    here = sums[:, 0:outputs, bass.ds(i * (2 * WINDOW) + (q - 2) * WINDOW, WINDOW)]
                    dve.wait_ge(ev["window"][q], more)
                    v.tensor_tensor(here, here, ps[:, 0:outputs, :], ALU.add)\
                        .then_inc(ev["added"][q], 1)
            dve.sem_inc(sm["window"], 1)
            dve.wait_ge(ev["added"][1], h.number(all_windows // 2, all_windows // 2 + 1))
            dve.sem_inc(sm["added"], 1)

        def layer0_any(h):
            if h.counter.eng is None and h.rel == 0:
                for part in range(2):
                    squared_lengths(part)
            cap0(h)
            soft0(h)
            msg0(h)
            every_window(L0, every[0], h, 1)

        def layer1_any(h):
            msg1(h)
            every_window(L1, every[1], h, 2)

        dve.wait_ge(d_bases, 16)
        dve.wait_ge(s_flag, 2)
        flag = dve.value_load(sorted_flag[0:1, 0:1], min_val=0, max_val=1)
        with dve.If(flag):
            loop_layer(layer0, 6)
        with dve.Else():
            for q in range(2):
                dve.sem_inc(every[0]["window"][q], 1)
                dve.sem_inc(every[0]["added"][q], 1)
            for_halves(dve, iterations, layer0_any, 0)

        for nm in (norm0, norm1):
            dve.sem_inc(nm["dve"], WIDE)

        def statistics(nm, u, source):
            rows, w = slice(0, u.rows), u.wide_slot
            dve.sem_inc(nm["begun"], 1)
            for t in range(u.tiles):
                last = v.bn_stats(stats[rows, w, t, :], source[rows, t, :])
            last.then_inc(nm["stats"], 1)

        def moments_of(nm, u):
            rows, w = slice(0, u.rows), u.wide_slot
            wait(dve, nm["stats"], u.upto())
            dve.sem_inc(nm["begun"], 1)
            for t in range(u.tiles):
                last = v.bn_aggr(mean_var[rows, w, t, :], stats[rows, w, t, :])
            last.then_inc(nm["moments"], 1)

        def offsets(nm, u):
            rows, w, q = slice(0, u.rows), u.wide_slot, slice(0, u.tiles)
            wait(dve, nm["inverse"], u.upto())
            v.scalar_tensor_tensor(out=offset[rows, w, q], in0=mean_var[rows, w, q, 0],
                                   scalar=-1.0, in1=inverse[rows, w, q], op0=ALU.mult,
                                   op1=ALU.mult)

        def normalise(nm, u, source, target):
            rows, w = slice(0, u.rows), u.wide_slot
            for t in range(act_from(nm, u)):
                last = v.tensor_scalar(target(t), source[rows, t, :], mean_var[rows, w, t, 0:1],
                                       inverse[rows, w, t:t + 1], ALU.subtract, ALU.mult)
            last.then_inc(nm["dve"], 1)

        def dense(back):
            m = back(3)
            if m is not None:
                wait(dve, dense0["added"], m.upto())
                statistics(norm0, m, outps[m.wide_slot])
            u = back(0)
            if u is not None:
                n = u.cols
                wait(dve, dense0["hidden"], u.upto(2))
                wait(dve, dense0["first"], u.upto())
                v.tensor_scalar(soft[:, u.slot, 0:n], filtA[u.slot][:, 0:n], bm1_c, EXP_CAP,
                                ALU.add, ALU.min).then_inc(dense0["capped"], 1)
            if m is not None:
                moments_of(norm0, m)
            u = back(1)
            if u is not None:
                n = u.cols
                wait(dve, dense0["soft_l"], u.upto())
                wait(dve, dense0["second"], u.upto(2))
                v.scalar_tensor_tensor(out=hid[:, u.slot, 0:n], in0=filtA[u.slot][:, 0:n],
                                       scalar=bm1_s, in1=soft[:, u.slot, 0:n], op0=ALU.add,
                                       op1=ALU.max).then_inc(dense0["hidden"], 1)
            f = back(4)
            if f is not None:
                offsets(norm0, f)
                normalise(norm0, f, outps[f.wide_slot], lambda t: row_tile(f, t))
        dve.wait_ge(d_up, 16 * 18)
        out_scale = 1.0 / (math.sqrt(2 * MUL) * AVG_DEGREE)
        root3 = math.sqrt(3.0)
        for k, w_sb in enumerate((W_outA, W_outB)):
            v.tensor_scalar(w_sb[0:MUL, 0:MUL], W_out_in[0:MUL, k, :], out_scale, None, ALU.mult)
            for c in range(3):
                cs = slice(MUL * (c + 1), MUL * (c + 2))
                last = v.tensor_scalar(w_sb[cs, MUL + c:P:3], W_out_in[cs, k, :],
                                       out_scale * (root3 if k else 1.0), None, ALU.mult)
        last.then_inc(s_weights, 1)
        for_units(dve, nodes, dense, 4)

        def copy_rows(u):
            rows = slice(0, u.rows)
            wait(dve, norm0["dve"], u.upto(-WIDE))
            wait(dve, norm0["act"], u.upto(-WIDE))
            wait(dve, table1["turned"], u.upto(WIDE))
            v.tensor_scalar(unit_in[rows, u.wide_slot, 0:u.tiles, :],
                            x_sb[rows, at(u.tile(), u.tiles), :], 1.0, None, ALU.mult)\
                .then_inc(table1["normed"], 1)
        each_unit(dve, nodes, copy_rows)

        dve.wait_ge(s_norm, 3)
        then(v.tensor_scalar(norm, norm, 1e-12, None, ALU.add))
        then(v.reciprocal(norm, norm))
        then(v.tensor_tensor(raw.rearrange("p (e c) -> p e c", c=3),
                             raw.rearrange("p (e c) -> p e c", c=3),
                             norm.rearrange("p (e a) -> p e a", a=1)
                             .broadcast_to([P, all_chunks, 3]), ALU.mult))

        dve.wait_ge(s_zeroed, 1)
        flag = dve.value_load(sorted_flag[0:1, 0:1], min_val=0, max_val=1)
        with dve.If(flag):
            loop_layer(layer1, 6)
        with dve.Else():
            for q in range(2):
                dve.sem_inc(every[1]["window"][q], 1)
                dve.sem_inc(every[1]["added"][q], 1)
            for_halves(dve, iterations, layer1_any, 0)

        def finish(back):
            u, f = back(0), back(1)
            if u is not None:
                wait(dve, dense1["added"], u.upto())
                statistics(norm1, u, outps[u.wide_slot])
            if f is not None:
                offsets(norm1, f)
                wait(dve, s_out[f.wide_slot], f.uses(16))
                normalise(norm1, f, outps[f.wide_slot],
                          lambda t: rows_out[f.wide_slot][0:f.rows, t, :])
            if u is not None:
                moments_of(norm1, u)
        for_units(dve, nodes, finish, 1)


def kernel(**inputs):
    import concourse.bacc as bacc
    from concourse.bass_utils import run_bass_kernel_spmd

    x = np.ascontiguousarray(inputs["x"])
    nodes = x.shape[0]
    edges = inputs["src"].shape[0]
    more = padded_edges(edges) - edges
    arrays = {"x": x}
    for name, fill in (("src", 0), ("dst", pad_receiver(nodes)), ("edge_attr_3", 0),
                       ("edge_weight", 0)):
        a = np.asarray(inputs[name])
        tail = np.full((more,) + a.shape[1:], fill, a.dtype)
        arrays[name] = np.ascontiguousarray(np.concatenate([a, tail]))
    for name in ("L0_gnn_W_lin", "L0_gnn_Wf1", "L0_gnn_bf1", "L0_gnn_Wf2", "L0_gnn_bf2",
                 "L0_gnn_Wm1", "L0_gnn_bm1", "L0_gnn_Wm2", "L0_gnn_bm2", "L1_gnn_W_up0",
                 "L1_gnn_W_up1", "L1_gnn_mlp_w0", "L1_gnn_mlp_b0", "L1_gnn_mlp_w1",
                 "L1_gnn_mlp_b1", "L1_gnn_mlp_w2", "L1_gnn_mlp_b2", "L1_gnn_W_out0",
                 "L1_gnn_W_out1"):
        arrays[name] = np.ascontiguousarray(inputs[name])
    nc = bacc.Bacc("TRN2", target_bir_lowering=False, num_devices=1)
    args = [nc.dram_tensor(f"in_{k}", a.shape, mybir.dt.from_np(a.dtype), kind="ExternalInput").ap()
            for k, a in arrays.items()]
    args.append(nc.dram_tensor("out", x.shape, F32, kind="ExternalOutput").ap())
    with ExitStack() as ctx:
        build(nc, *args, ctx)
    r = run_bass_kernel_spmd(nc, [{f"in_{k}": a for k, a in arrays.items()}], core_ids=[0])
    return r.results[0]["out"]
```
